# Optimizing a Trainium2 kernel written in Bass

```python
import numpy as np
import jax
import jax.numpy as jnp

def _softmax(x, axis=-1):
    return jax.nn.softmax(x, axis=axis)

def _gelu(x):
    return jax.nn.gelu(x, approximate=True)

def _silu(x):
    return jax.nn.silu(x)

def _sigmoid(x):
    return jax.nn.sigmoid(x)

def _layernorm(x, axis=-1, eps=1e-05):
    m = jnp.mean(x, axis=axis, keepdims=True)
    v = jnp.var(x, axis=axis, keepdims=True)
    return (x - m) / jnp.sqrt(v + eps)

def _scatter_add(tgt, idx, src, axis=0):
    return tgt.at[idx].add(src)

def _segment_sum(src, seg, n):
    return jax.ops.segment_sum(src, seg, n)
kernel_name = 'mk_prb_d1_jaxref_r4_7eaeff'

def setup_inputs(seed: int=0):
    np.random.seed(seed)
    _w = jnp.asarray

    def _L0_attn_setup():
        import jax, jax.numpy as jnp
        import numpy as np
        EPS = 1e-12

        def _l2norm(t, axis=-1):
            return t / jnp.maximum(jnp.linalg.norm(t, axis=axis, keepdims=True), EPS)

        def _selective_scan(u, delta, A, Bm, Cm, D):
            uT = u.transpose(2, 0, 1)
            dT = delta.transpose(2, 0, 1)
            BT = Bm.transpose(2, 0, 1)
            CT = Cm.transpose(2, 0, 1)
            h0 = jnp.zeros(u.shape[:2] + (A.shape[1],), u.dtype)

            def step(h, inp):
                u_t, d_t, b_t, c_t = inp
                dA = jnp.exp(d_t[..., None] * A)
                h = dA * h + (d_t * u_t)[..., None] * b_t[:, None, :]
                y = jnp.einsum('bdn,bn->bd', h, c_t)
                return (h, y)
            _, ys = jax.lax.scan(step, h0, (uT, dT, BT, CT))
            y = ys.transpose(1, 2, 0)
            return y + D[None, :, None] * u
        key = jax.random.key(seed)
        ks = jax.random.split(key, 8)
        B, N, d_inner, d_state, dt_rank, K = (8, 512, 256, 16, 32, 8)
        x = jax.random.normal(ks[0], (B, N, d_inner), jnp.float32)
        means = jax.random.normal(ks[1], (K, d_inner), jnp.float32)
        prompt_weight = jax.random.normal(ks[2], (d_state, d_inner), jnp.float32) * d_inner ** (-0.5)
        x_proj_weight = jax.random.normal(ks[3], (dt_rank + 2 * d_state, d_inner), jnp.float32) * d_inner ** (-0.5)
        dt_init_std = dt_rank ** (-0.5)
        dt_projs_weight = jax.random.uniform(ks[4], (d_inner, dt_rank), jnp.float32, -dt_init_std, dt_init_std)
        dt = jnp.exp(jax.random.uniform(ks[5], (d_inner,), jnp.float32) * (np.log(0.1) - np.log(0.001)) + np.log(0.001))
        dt = jnp.clip(dt, 0.0001, None)
        dt_projs_bias = dt + jnp.log(-jnp.expm1(-dt))
        A_logs = jnp.log(jnp.broadcast_to(jnp.arange(1, d_state + 1, dtype=jnp.float32), (d_inner, d_state)))
        Ds = jnp.ones((d_inner,), jnp.float32)
        return {'x': x, 'means': means, 'prompt_weight': prompt_weight, 'x_proj_weight': x_proj_weight, 'dt_projs_weight': dt_projs_weight, 'dt_projs_bias': dt_projs_bias, 'A_logs': A_logs, 'Ds': Ds}
    _L0_attn_in = _L0_attn_setup()

    def _L0_ffn_setup():
        import jax, jax.numpy as jnp
        import numpy as np
        B, S, D = (4, 512, 256)
        E, H, TOP_K = (8, 512, 2)
        key = jax.random.key(seed)
        k_x, k_g, k_w1, k_w2, k_w3 = jax.random.split(key, 5)
        s_d = 1.0 / np.sqrt(D)
        s_h = 1.0 / np.sqrt(H)
        return {'x': jax.random.normal(k_x, (B, S, D), dtype=jnp.float32), 'w_gate': jax.random.normal(k_g, (D, E), dtype=jnp.float32) * s_d, 'w1': jax.random.normal(k_w1, (E, D, H), dtype=jnp.float32) * s_d, 'w3': jax.random.normal(k_w3, (E, D, H), dtype=jnp.float32) * s_d, 'w2': jax.random.normal(k_w2, (E, H, D), dtype=jnp.float32) * s_h}
    _L0_ffn_in = _L0_ffn_setup()
    _d = {'L0_attn_x': _L0_attn_in['x'], 'L0_attn_means': _L0_attn_in['means'], 'L0_attn_prompt_weight': _L0_attn_in['prompt_weight'], 'L0_attn_x_proj_weight': _L0_attn_in['x_proj_weight'], 'L0_attn_dt_projs_weight': _L0_attn_in['dt_projs_weight'], 'L0_attn_dt_projs_bias': _L0_attn_in['dt_projs_bias'], 'L0_attn_A_logs': _L0_attn_in['A_logs'], 'L0_attn_Ds': _L0_attn_in['Ds'], 'L0_ffn_w_gate': _L0_ffn_in['w_gate'], 'L0_ffn_w1': _L0_ffn_in['w1'], 'L0_ffn_w3': _L0_ffn_in['w3'], 'L0_ffn_w2': _L0_ffn_in['w2']}
    _x0 = _d['L0_attn_x']
    _d['L0_attn_x'] = jax.random.normal(jax.random.fold_in(jax.random.key(seed), 1), (2, 2048, 256), dtype=_x0.dtype)
    del _x0
    return _d

def reference(L0_attn_x, L0_attn_means, L0_attn_prompt_weight, L0_attn_x_proj_weight, L0_attn_dt_projs_weight, L0_attn_dt_projs_bias, L0_attn_A_logs, L0_attn_Ds, L0_ffn_w_gate, L0_ffn_w1, L0_ffn_w3, L0_ffn_w2):

    def _L0_attn_ref(x, means, prompt_weight, x_proj_weight, dt_projs_weight, dt_projs_bias, A_logs, Ds):
        import jax, jax.numpy as jnp
        import numpy as np
        EPS = 1e-12

        def _l2norm(t, axis=-1):
            return t / jnp.maximum(jnp.linalg.norm(t, axis=axis, keepdims=True), EPS)

        def _selective_scan(u, delta, A, Bm, Cm, D):
            uT = u.transpose(2, 0, 1)
            dT = delta.transpose(2, 0, 1)
            BT = Bm.transpose(2, 0, 1)
            CT = Cm.transpose(2, 0, 1)
            h0 = jnp.zeros(u.shape[:2] + (A.shape[1],), u.dtype)

            def step(h, inp):
                u_t, d_t, b_t, c_t = inp
                dA = jnp.exp(d_t[..., None] * A)
                h = dA * h + (d_t * u_t)[..., None] * b_t[:, None, :]
                y = jnp.einsum('bdn,bn->bd', h, c_t)
                return (h, y)
            _, ys = jax.lax.scan(step, h0, (uT, dT, BT, CT))
            y = ys.transpose(1, 2, 0)
            return y + D[None, :, None] * u
        dt_rank = dt_projs_weight.shape[1]
        d_state = A_logs.shape[1]
        scores = jnp.einsum('bnd,kd->bnk', _l2norm(x), _l2norm(means))
        buckets = jnp.argmax(jax.lax.stop_gradient(scores), axis=-1)
        sort_idx = jnp.argsort(buckets, axis=-1, stable=True)
        inv_idx = jnp.argsort(sort_idx, axis=-1)
        xs = jnp.take_along_axis(x, sort_idx[..., None], axis=1)
        b_sorted = jnp.take_along_axis(buckets, sort_idx, axis=1)
        cluster_prompts = means @ prompt_weight.T
        prompt = cluster_prompts[b_sorted]
        u = xs.transpose(0, 2, 1)
        x_dbl = jnp.einsum('bdl,cd->bcl', u, x_proj_weight)
        dts = x_dbl[:, :dt_rank]
        Bm = x_dbl[:, dt_rank:dt_rank + d_state]
        Cm = x_dbl[:, dt_rank + d_state:] + prompt.transpose(0, 2, 1)
        delta = jax.nn.softplus(jnp.einsum('brl,dr->bdl', dts, dt_projs_weight) + dt_projs_bias[None, :, None])
        A = -jnp.exp(A_logs)
        y = _selective_scan(u, delta, A, Bm, Cm, Ds)
        y = y.transpose(0, 2, 1)
        out = jnp.take_along_axis(y, inv_idx[..., None], axis=1)
        return out

    def _L0_ffn_ref(x, w_gate, w1, w3, w2):
        import jax, jax.numpy as jnp
        import numpy as np
        B, S, D = (4, 512, 256)
        E, H, TOP_K = (8, 512, 2)
        bsz, seq_len, embed_dim = x.shape
        xt = x.reshape(-1, embed_dim)
        T = xt.shape[0]
        logits = xt @ w_gate
        top_logits, sel = jax.lax.top_k(logits, TOP_K)
        probs = jax.nn.softmax(top_logits, axis=-1).astype(x.dtype)
        h = jax.nn.silu(jnp.einsum('td,edh->eth', xt, w1)) * jnp.einsum('td,edh->eth', xt, w3)
        y = jnp.einsum('eth,ehd->etd', h, w2)
        t_idx = jnp.arange(T)
        yk = y[sel.T, t_idx[None, :], :]
        out = jnp.einsum('ktd,tk->td', yk, probs)
        return out.reshape(bsz, seq_len, embed_dim)
    x = L0_attn_x
    xn = _layernorm(x, axis=-1)
    x = x + _L0_attn_ref(xn, L0_attn_means, L0_attn_prompt_weight, L0_attn_x_proj_weight, L0_attn_dt_projs_weight, L0_attn_dt_projs_bias, L0_attn_A_logs, L0_attn_Ds) + _L0_ffn_ref(xn, L0_ffn_w_gate, L0_ffn_w1, L0_ffn_w3, L0_ffn_w2)
    return x

_drawn_inputs = setup_inputs


def setup_inputs(seed=0):
    import zlib

    import numpy as np

    out = dict(_drawn_inputs(seed))
    spreads = {'L0_attn_Ds': (1.0, 0.2)}
    factors = {}
    for name, (base, spread) in spreads.items():
        noise = np.random.default_rng([zlib.crc32(name.encode()), seed]).standard_normal(out[name].shape)
        drawn = base * np.exp(spread * noise) if base else spread * noise
        out[name] = jnp.asarray(drawn.astype(out[name].dtype))
    for name, factor in factors.items():
        out[name] = (out[name] * factor).astype(out[name].dtype)
    return out
```

```python
from contextlib import ExitStack

import concourse.bass as bass
from concourse import mybir

F32 = mybir.dt.float32
U32 = mybir.dt.uint32
I32 = mybir.dt.int32
ALU = mybir.AluOpType
ACT = mybir.ActivationFunctionType
AX = mybir.AxisListType.X

P = 128
BATCH, LEN, D = 2, 2048, 256
TOK = BATCH * LEN
NT = TOK // P
KC = D // P
NB = 8
NS, DTR = 16, 32
NX = DTR + 2 * NS
E, H = 8, 512
HC = H // P
ROWW = D + 2
FT = (2 * TOK) // P + E - 1
FTP = FT + 1
CH = 512
NCH = TOK // CH
CPB = LEN // CH
TPC = CH // P
DG = 32
G = D // DG
NH = 4
RING = 4
SPI = 10
TURNS = NCH - 1
EPS_LN, EPS_NORM = 1e-5, 1e-12
BIG = 3.0e38

UNIT_OF_STEP = {0: 0, 1: 1, 2: 2, 3: 3, 5: 4, 6: 5, 7: 6, 8: 7}



def program(nc, x_in, means_in, prompt_in, xproj_in, dtw_in, dtb_in, alog_in, ds_in, gate_in, w1_in, w3_in, w2_in, out):
    with ExitStack() as ctx:
        def sb(name, shape, dt=F32):
            return ctx.enter_context(nc.sbuf_tensor(name, shape, dt))

        def sem(name):
            return ctx.enter_context(nc.semaphore(name))

        def dram(name, shape):
            return nc.dram_tensor(name, shape, F32, kind="Internal").ap()

        xs_d = dram("xs_d", [TOK, ROWW])
        xe_d = dram("xe_d", [FTP * P, ROWW])
        bc_d = dram("bc_d", [NCH, 2 * NS, CH])
        dd_d = dram("dd_d", [NCH * D, 2 * CH])
        acc_d = dram("acc_d", [TOK, D])
        y_d = dram("y_d", [2 * TOK + 2 * P, D])

        ring = sb("ring", [P, RING, NH, CH])
        bc = sb("bc", [P, 2, 2, NH, CH])
        late = sb("late", [P, 2 * 2 * CH + 2 * TPC * D])
        dd = late[:, 0:2048].rearrange("p (s r c) -> p s r c", s=2, r=2)
        w1 = sb("w1", [P, E * KC * H])
        w3 = sb("w3", [P, E * KC * H])
        w2x = sb("w2x", [P, NT * ROWW])
        w2 = w2x[:, 0:E * HC * D]
        row = w2x[:, :].rearrange("p (t c) -> p t c", c=ROWW)
        row_u = row.bitcast(U32)
        ya = late[:, 2048:3072].rearrange("p (t c) -> p t c", t=TPC)
        yb = late[:, 3072:4096].rearrange("p (t c) -> p t c", t=TPC)
        idb = sb("idb", [P, TPC], U32)
        ids = sb("ids", [P, NT], U32)
        state = sb("state", [P, G * NH])
        keep = sb("keep", [P, NCH])
        aneg = sb("aneg", [P, G * NH])
        ident = sb("ident", [P, P])
        fold = sb("fold", [P, DG])
        y1 = sb("y1", [P, P])
        meta = sb("meta", [P, SPI, 2])
        etab = sb("etab", [1, FTP], I32)

        pool = sb("pool", [P, 5128])
        xr = pool[:, 0:512].rearrange("p (s c) -> p s c", s=2)
        xt = pool[:, 512:1024].rearrange("p (s c) -> p s c", s=2)
        sg = pool[:, 1024:2048].rearrange("p (s c) -> p s c", s=2)
        ht = pool[:, 2048:2560]
        ye = pool[:, 2560:3072].rearrange("p (s c) -> p s c", s=2)
        xsr = pool[:, 0:TPC * ROWW].rearrange("p (t c) -> p t c", c=ROWW)
        ut = pool[:, 1032:2056].rearrange("p (k c) -> p k c", k=KC)
        xd = pool[:, 2056:2568]
        el = [pool[:, 2568:3080], late[:, 3072:3584]]
        ddst = [pool[:, 3080:4104].rearrange("p (k c) -> p k c", k=2), pool[:, 4104:5128].rearrange("p (k c) -> p k c", k=2)]
        over = late[0:NB, 3584:4096]
        osort = sb("osort", [NB, CH])[:, :]
        iota512 = sb("iota512", [NB, CH])

        xprojT = sb("xprojT", [P, KC, NX])
        dtwT = sb("dtwT", [DTR, D])
        dtb = sb("dtb", [1, D])
        one_row = sb("one_row", [1, CH])
        cpT = sb("cpT", [NB, NX])
        lo_c = sb("lo_c", [NB, NCH])
        hi_c = sb("hi_c", [NB, NCH])
        prob2 = sb("prob2", [P, NT])
        pos_a = sb("pos_a", [P, NT], U32)
        pos_1 = sb("pos_1", [P, NT], U32)
        pos_2 = sb("pos_2", [P, NT], U32)

        xin = ring[:, :, :, :].rearrange("p a b c -> p (a b c)").rearrange("p (t c) -> p t c", c=D)
        tmp = bc[:, :, :, :, :].rearrange("p a b c d -> p (a b c d)")
        room = [[tmp, 0, 2 * 2 * NH * CH], [late, 0, 4096]]

        def cut(n, parts=P):
            r = room[0] if room[0][1] + n <= room[0][2] else room[1]
            a = r[1]
            r[1] += n
            assert r[1] <= r[2]
            return r[0][0:parts, a:a + n]

        xnT = cut(2 * KC * CH).rearrange("p (s k c) -> p s k c", s=2, k=KC)
        lg = cut(NT * 16).rearrange("p (t c) -> p t c", c=16)
        pad = cut(2 * ROWW).rearrange("p (s c) -> p s c", s=2)
        dsb = cut(D)
        ones = cut(2 * NB * NT)
        tri = cut(P)
        wg = cut(KC * 16).rearrange("p (k c) -> p k c", k=KC)
        nat = cut(D * 3 + 64)
        stats = cut(TPC * 6).rearrange("p (t c) -> p t c", c=6)
        mv = cut(TPC * 2).rearrange("p (t c) -> p t c", c=2)
        sd = cut(TPC)
        rs = cut(TPC)
        rt = cut(TPC)
        var = cut(NT)
        rstd = cut(NT)
        rn = cut(NT)
        km8 = cut(NB)
        mk = cut(2 * NT * NB).rearrange("p (a t k) -> p a t k", a=2, k=NB)
        o1 = cut(NT * NB).rearrange("p (t k) -> p t k", k=NB)
        o2 = cut(NT * NB).rearrange("p (t k) -> p t k", k=NB)
        sc = cut(NT * NB).rearrange("p (t k) -> p t k", k=NB)
        l2 = cut(NT * NB).rearrange("p (t k) -> p t k", k=NB)
        eq = cut(NT * NB).rearrange("p (t k) -> p t k", k=NB)
        mx = cut(NT)
        m1 = cut(NT)
        m2 = cut(NT)
        mn8 = cut(NT)
        pr = cut(NT)
        cn = cut(2 * NT * NB)
        cs = cut(2 * NT * NB)
        ex = cut(2 * NT * NB)
        adr = cut(2 * NT * NB).rearrange("p (a t k) -> p a t k", a=2, k=NB)
        tl = cut(NB)
        ct = cut(NB)
        off = cut(NB)
        tli = cut(NB)
        posf = cut(NT)
        jt = cut(FTP, 1)
        ge = cut(FTP * NB, 1).rearrange("p (j k) -> p j k", k=NB)
        etf = cut(FTP, 1)
        lo2 = cut(BATCH * NB, NB).rearrange("p (b k) -> p b k", b=BATCH)
        lo1 = cut(BATCH, NB)
        hi1 = cut(BATCH, NB)
        c512 = cut(NCH, NB)
        mnat = nat[0:NB, 0:D]
        mnrm = nat[0:NB, D:2 * D]
        mjunk = nat[0:NB, 2 * D:3 * D]
        msum = nat[0:NB, 3 * D:3 * D + 1]
        mrec = nat[0:NB, 3 * D + 1:3 * D + 2]
        pnat = cut(D, NS)
        xpnat = cut(D, NX)
        dtnat = cut(KC * DTR).rearrange("p (k r) -> p k r", k=KC)
        mT = cut(KC * NB).rearrange("p (k r) -> p k r", k=KC)
        pT = cut(KC * NS).rearrange("p (k r) -> p k r", k=KC)
        skip = pool[:, 0:TPC * D].rearrange("p (t c) -> p t c", c=D)

        def ps(name, cols):
            return ctx.enter_context(nc.psum_tensor(name, [P, cols], F32))

        pb = ps("pb", 1024)
        fa = [ps("fa0", 512), ps("fa1", 512)]
        fb = [ps("fb0", 512), ps("fb1", 512)]
        pt = ps("pt", 512)
        py = ps("py", 512)

        names = """passed x_in0 x_in1 const_in pad_ready pad_put w13_in w2_in ln_stats ln_sd ln_rows ln_tr ln_ev
        ln_mm acc_ready acc_put pool_const dve_const small_tr small_cp cp_ready norm_sq norm_sqrt
        norm_ready sqrt_v sqrt_done chain masks_ready ranks_ready gap_ready exp_gap probs_ready pos_ready
        ffn_pos_ready pool_step xs_put0 xs_put1 xe_put1 xe_put2 aneg_exp
        xs_in pr_tr pr_ut pr_os pr_x pr_xd pr_dp pr_ab pr_ex pr_ln pr_de pr_du bc_put dd_put0 dd_put1 pr_ids
        bc_in dd_in0 dd_in1 exp_done dbu_done scan_done keep_done h_ready hc_done sum_done y1_done ytr_done
        ya_done yb_done idb_done
        xr_in0 xr_in1 xtr_done xt_done a_done b_done tanh_done s1_done silu_done htr_done ht_done w2_done ye_done
        out_ready out_put ye_put0 ye_put1 yb_put parts_in0 parts_in1 parts_in2 parts_in3 parts_in4 parts_in5 parts_in6
        parts_in7""".split()
        S = {n: sem(n) for n in names}
        x_sem = [S["x_in0"], S["x_in1"]]
        dd_in = [S["dd_in0"], S["dd_in1"]]
        xr_in = [S["xr_in0"], S["xr_in1"]]

        block = ctx.enter_context(nc.Block())

        def apart(eng):
            eng.sem_inc(S["passed"], 1)

        def unit_index(chunk, g):
            return chunk * G + g

        @block.sync
        def _(sp):
            x_v = x_in.rearrange("b (q j p) d -> (b q) p j d", p=P, j=TPC)
            for h in range(2):
                sp.dma_start(xin[:, TPC * h:TPC * h + TPC, :], x_v[h]).then_inc(x_sem[h], 16)
            with sp.Fori(1, NCH // 2) as i:
                for h in range(2):
                    sp.wait_ge(x_sem[h], 16 * i)
                    apart(sp)
                    sp.dma_start(xin[:, bass.ds(8 * i + 4 * h, TPC), :],
                                 x_v[bass.ds(2 * i + h, 1), :, :, :].rearrange("o p j d -> (o p) j d")).then_inc(x_sem[h], 16)
            sp.wait_ge(S["pad_ready"], 3)
            for s in range(2):
                sp.dma_start(xe_d.rearrange("(t s p) c -> s p t c", p=P, s=2)[s],
                             pad[:, s:s + 1, :].to_broadcast([P, FTP // 2, ROWW])).then_inc(S["pad_put"], 16)
            with sp.Fori(0, E) as e:
                for w, src in ((w1, w1_in), (w3, w3_in)):
                    sp.dma_start(w[:, bass.ds(e * (KC * H), KC * H)].rearrange("p (k h) -> p k h", k=KC),
                                 src[bass.ds(e, 1), :, :].rearrange("o (k p) h -> (o p) k h", p=P)).then_inc(S["w13_in"], 16)
            acc_v = acc_d.rearrange("(q j p) d -> q p j d", p=P, j=TPC)
            for q in range(NCH):
                sp.wait_ge(S["acc_ready"], q + 2)
                sp.dma_start(acc_v[q], xin[:, TPC * q:TPC * q + TPC, :]).then_inc(S["acc_put"], 16)

            xs_v = xs_d.rearrange("(q j p) c -> q p j c", p=P, j=TPC)

            def load_sorted(c):
                sp.wait_ge(S[f"xs_put{c // CPB}"], 16 * NT // BATCH)
                if c == 0:
                    sp.wait_ge(S["acc_ready"], NCH + 1)
                else:
                    sp.wait_ge(S["pr_tr"], c)
                    sp.wait_ge(S["pr_ids"], c)
                sp.dma_start(xsr, xs_v[c]).then_inc(S["xs_in"], 16)

            def store_dd(c):
                for h in range(KC):
                    sp.wait_ge(S["pr_du"], KC * c + h + 1)
                    sp.dma_start(dd_d[D * c + P * h:D * c + P * h + P, :],
                                 ddst[h].rearrange("p k c -> p (k c)")).then_inc(S[f"dd_put{h}"], 16)

            def load_dd(c, g):
                if not (isinstance(c, int) and c == 0 and g < 2):
                    sp.wait_ge(S["exp_done"], unit_index(c, g) - 1)
                    apart(sp)
                    sp.wait_ge(S["dbu_done"], 2 * (unit_index(c, g) - 1))
                apart(sp)
                for q in range(P // DG):
                    sp.dma_start(dd[DG * q:DG * q + DG, g % 2, :, :].rearrange("p k c -> p (k c)"),
                                 dd_d[bass.ds(unit_index(c, g) * DG, DG), :]).then_inc(dd_in[g % 2], 16)

            def load_bc(c, parity):
                for q in range(P // DG):
                    for r in range(2):
                        n = r * NS + NH * q
                        src = bc_d[bass.ds(c, 1), n:n + NH, :].rearrange("o n c -> o (n c)").to_broadcast([DG, NH * CH])
                        sp.dma_start(bc[DG * q:DG * q + DG, parity, r, :, :] if isinstance(parity, int) else
                                     bc[DG * q:DG * q + DG, bass.ds(parity, 1), r, :, :], src).then_inc(S["bc_in"], 16)

            def load_w2():
                sp.wait_ge(S["xe_put1"], 16 * NT)
                sp.wait_ge(S["xe_put2"], 16 * NT)
                for e in range(E):
                    sp.dma_start(w2[:, e * HC * D:(e + 1) * HC * D].rearrange("p (k d) -> p k d", k=HC),
                                 w2_in[e].rearrange("(k p) d -> p k d", p=P)).then_inc(S["w2_in"], 16)

            load_sorted(0)
            store_dd(0)
            sp.wait_ge(S["dd_put0"], 16)
            sp.wait_ge(S["dd_put1"], 16)
            load_dd(0, 0)
            sp.wait_ge(S["bc_put"], 16)
            load_bc(0, 0)
            load_dd(0, 1)
            load_sorted(1)
            for k in range(G):
                if 0 < k < G - 1:
                    load_dd(0, k + 1)
                if k + 2 < NCH:
                    load_sorted(k + 2)
                if k + 1 < NCH:
                    store_dd(k + 1)
                if k == 3:
                    load_w2()
                if k == 2:
                    sp.wait_ge(S["bc_put"], 32)
                    sp.wait_ge(S["bc_in"], 128)
                    load_bc(1, 1)
            sp.wait_ge(S["dd_put0"], 16 * NCH)
            sp.wait_ge(S["dd_put1"], 16 * NCH)
            sp.wait_ge(S["bc_put"], 16 * NCH)

            xe_v = xe_d.rearrange("(t p) c -> t p c", p=P)

            def load_tile(j, parity, slot):
                v = xe_v[bass.ds(j, 1), :, :].rearrange("o p c -> (o p) c")
                sp.dma_start(xr[:, parity, :], v[:, 0:D]).then_inc(xr_in[parity], 16)
                sp.dma_start(meta[:, slot, :], v[:, D:ROWW]).then_inc(xr_in[parity], 16)

            sp.wait_ge(S["pr_du"], KC * NCH)
            load_tile(0, 0, 0)
            load_tile(1, 1, 1)
            with sp.Fori(0, TURNS) as i:
                for s in range(SPI):
                    j = SPI * i + 1 + s
                    k = UNIT_OF_STEP.get(s)
                    if k is not None:
                        load_dd(i + 1, k)
                        if k == 3:
                            sp.wait_ge(S["hc_done"], G * (i + 1))
                            apart(sp)
                            sp.wait_ge(S["bc_in"], 128 * (i + 2))
                            apart(sp)
                            load_bc((i + 2) % NCH, i % 2)
                    sp.wait_ge(S["xtr_done"], j)
                    apart(sp)
                    load_tile(j + 1, s % 2, (s + 2) % SPI)
            sp.wait_ge(S["w2_done"], FT)
            sp.wait_ge(S["yb_put"], 16 * (TPC * NCH + 1))
            sp.wait_ge(S["ye_put0"], 16 * ((FT + 1) // 2 + 1))
            sp.wait_ge(S["ye_put1"], 16 * (FT // 2 + 1))
            for q in range(NCH):
                for dst, src in ((w1, acc_d), (w3, y_d[0:TOK, :]), (w2, y_d[TOK:2 * TOK, :])):
                    sp.dma_start(dst[:, TPC * D * q:TPC * D * q + TPC * D],
                                 src.rearrange("(p r) d -> p (r d)", p=P)[:, TPC * D * q:TPC * D * q + TPC * D]).then_inc(S[f"parts_in{q}"], 16)
            for q in range(NCH):
                sp.wait_ge(S["out_ready"], 2 * q + 2)
                sp.dma_start(out.rearrange("b (p r) d -> (b p) (r d)", p=P // BATCH)[:, TPC * D * q:TPC * D * q + TPC * D],
                             w1[:, TPC * D * q:TPC * D * q + TPC * D]).then_inc(S["out_put"], 16)
            sp.wait_ge(S["bc_in"], 128 * (NCH + 1))
            sp.wait_ge(S["out_put"], 16 * NCH)

        @block.gpsimd
        def _(po):
            po.memset(ident[:, :], 0.0).then_inc(S["pool_step"], 1)
            po.memset(fold[:, :], 0.0).then_inc(S["pool_step"], 1)
            po.memset(tri, 1.0).then_inc(S["pool_step"], 1)
            po.wait_ge(S["pool_step"], 3)
            po.affine_select(out=ident[:, :], in_=ident[:, :], compare_op=ALU.not_equal, fill=1.0, base=0,
                             pattern=[[-1, P]], channel_multiplier=1).then_inc(S["pool_const"], 1)
            for q in range(P // DG):
                po.affine_select(out=fold[:, :], in_=fold[:, :], compare_op=ALU.not_equal, fill=1.0, base=-DG * q,
                                 pattern=[[-1, DG]], channel_multiplier=1).then_inc(S["pool_step"], 1)
                po.wait_ge(S["pool_step"], 4 + q)
            po.affine_select(out=tri, in_=tri, compare_op=ALU.is_gt, fill=0.0, base=0,
                             pattern=[[1, P]], channel_multiplier=-1).then_inc(S["pool_const"], 1)
            po.iota(row_u.bitcast(I32)[:, :, D:D + 1], [[P, NT], [0, 1]], base=0, channel_multiplier=1).then_inc(S["pool_const"], 1)
            po.iota(pad.bitcast(I32)[:, :, D:D + 1], [[P, 2], [0, 1]], base=2 * TOK, channel_multiplier=1).then_inc(S["pad_ready"], 1)
            po.iota(km8, [[1, NB]], base=-NB, channel_multiplier=0, allow_small_or_imprecise_dtypes=True).then_inc(S["pool_const"], 1)
            po.iota(jt, [[1, FTP]], base=0, channel_multiplier=0, allow_small_or_imprecise_dtypes=True).then_inc(S["pool_const"], 1)
            po.iota(c512, [[CH, NCH]], base=0, channel_multiplier=0, allow_small_or_imprecise_dtypes=True).then_inc(S["pool_const"], 1)
            po.iota(iota512[:, :], [[1, CH]], base=0, channel_multiplier=0, allow_small_or_imprecise_dtypes=True).then_inc(S["pool_const"], 1)

            def scatter(dst, index, t, done):
                po.indirect_dma_start(dst[:, :], bass.IndirectOffsetOnAxis(ap=index[:, t:t + 1], axis=0),
                                      row[:, t, :], None).then_inc(done, 16)

            po.wait_ge(S["pad_ready"], 3)
            for at, end, name in ((0, 32, "yb_put"), (32, 80, "ye_put0"), (80, P, "ye_put1")):
                po.dma_start(y_d[2 * TOK + at:2 * TOK + end, :], pad[at:end, 0, 0:D]).then_inc(S[name], 16)
            po.wait_ge(S["pos_ready"], 1)
            po.wait_ge(S["probs_ready"], 1)
            po.wait_ge(S["ln_rows"], NT)
            po.wait_ge(S["pool_const"], 3)
            for t in range(NT):
                scatter(xs_d, pos_a, t, S[f"xs_put{t // (NT // BATCH)}"])
            po.wait_ge(S["ffn_pos_ready"], 1)
            po.wait_ge(S["pad_put"], 32)
            for t in range(NT):
                scatter(xe_d, pos_1, t, S["xe_put1"])
            po.wait_ge(S["xe_put1"], 16 * NT)
            po.wait_ge(S["xs_put0"], 16 * NT // BATCH)
            po.wait_ge(S["xs_put1"], 16 * NT // BATCH)
            po.tensor_copy(row[:, :, D + 1], prob2[:, :]).then_inc(S["pool_const"], 1)
            po.iota(row_u.bitcast(I32)[:, :, D:D + 1], [[P, NT], [0, 1]], base=TOK, channel_multiplier=1).then_inc(S["pool_const"], 1)
            po.wait_ge(S["pool_const"], 9)
            for t in range(NT):
                scatter(xe_d, pos_2, t, S["xe_put2"])

            def put_expert(j, slot, parity):
                po.wait_ge(S["ye_done"], j + 2)
                apart(po)
                po.indirect_dma_start(y_d[:, :], bass.IndirectOffsetOnAxis(ap=meta.bitcast(U32)[:, slot, 0:1], axis=0),
                                      ye[:, parity, :], None).then_inc(S[f"ye_put{parity}"], 16)

            def add_scan(c, n):
                po.wait_ge(S["yb_done"], c + 1)
                apart(po)
                po.indirect_dma_start(acc_d[:, :], bass.IndirectOffsetOnAxis(ap=idb[:, n:n + 1], axis=0), yb[:, n, :], None,
                                      compute_op=ALU.add).then_inc(S["yb_put"], 16)

            po.wait_ge(S["acc_put"], 16 * NCH)
            po.wait_ge(S["yb_put"], 16)
            with po.Fori(0, TURNS) as i:
                for s in range(SPI):
                    k = UNIT_OF_STEP.get(s)
                    if k is not None:
                        u = unit_index(i + 1, k)
                        po.wait_ge(S["h_ready"], u + 1)
                        apart(po)
                        c_rows = bc[:, bass.ds((i + 1) % 2, 1), 1, :, :].rearrange("p o n c -> p (o n c)")
                        r = ring[:, k % RING, :, :].rearrange("p n c -> p (n c)")
                        po.tensor_tensor(r, r, c_rows, ALU.mult).then_inc(S["hc_done"], 1)
                        if k in (3, 4, 5, 6):
                            add_scan(i, k - 3)
                    put_expert(SPI * i + s, s, s % 2)
            put_expert(FT - 1, (FT - 1) % SPI, (FT - 1) % 2)
            for n in range(TPC):
                add_scan(NCH - 1, n)
            po.wait_ge(S["yb_put"], 16 * (TPC * NCH + 1))
            po.wait_ge(S["ye_put0"], 16 * ((FT + 1) // 2 + 1))
            po.wait_ge(S["ye_put1"], 16 * (FT // 2 + 1))

        @block.scalar
        def _(ac):
            n_const = 0
            for dst, src in ((mnat, means_in), (pnat, prompt_in), (xpnat, xproj_in),
                             (dtnat, dtw_in.rearrange("(k p) r -> p k r", p=P)),
                             (dtb[:, :], dtb_in.rearrange("(o d) -> o d", o=1)),
                             (wg[:, :, NB:2 * NB], gate_in.rearrange("(k p) e -> p k e", p=P)),
                             (dsb, ds_in.rearrange("(o d) -> o d", o=1).to_broadcast([P, D]))):
                ac.dma_start(dst, src).then_inc(S["const_in"], 16)
                n_const += 16
            for q in range(P // DG):
                ac.dma_start(aneg[DG * q:DG * q + DG, :].rearrange("p (g n) -> p g n", g=G),
                             alog_in.rearrange("(g d) (q n) -> q d g n", d=DG, n=NH)[q]).then_inc(S["const_in"], 16)
                n_const += 16
            ac.wait_ge(S["const_in"], n_const)
            ac.wait_ge(S["norm_sq"], 1)
            ac.activation(mrec, msum, ACT.Sqrt).then_inc(S["norm_sqrt"], 1)
            ac.wait_ge(S["small_tr"], 1)
            ac.copy(xprojT[:, :, :].rearrange("p k c -> p (k c)"), pt[:, 0:128]).then_inc(S["small_cp"], 1)
            ac.copy(wg[:, :, 0:NB], pt[:, 128:144].rearrange("p (k r) -> p k r", k=KC)).then_inc(S["small_cp"], 1)
            ac.copy(mT, pt[:, 144:160].rearrange("p (k r) -> p k r", k=KC)).then_inc(S["small_cp"], 1)
            ac.copy(pT, pt[:, 160:192].rearrange("p (k r) -> p k r", k=KC)).then_inc(S["small_cp"], 1)
            ac.copy(dtwT[:, :], pt[0:DTR, 192:448]).then_inc(S["small_cp"], 1)
            ac.wait_ge(S["ln_mm"], 2)
            ac.wait_ge(S["dve_const"], 1)
            ac.copy(cpT[:, DTR + NS:NX], py[0:NB, 0:NS]).then_inc(S["cp_ready"], 1)
            with ac.Fori(0, NCH // 2) as i:
                for h in range(2):
                    q = 2 * i + h
                    ac.wait_ge(S["ln_stats"], q + 1)
                    ac.activation(sd, rt, ACT.Sqrt).then_inc(S["ln_sd"], 1)
                    ac.wait_ge(S["ln_tr"], q + 1)
                    ac.wait_ge(S["ln_mm"], q + 1)
                    for k, src in enumerate((fa[h], fb[h])):
                        ac.copy(xnT[:, h, k, :], src[:, :]).then_inc(S["ln_ev"], 1)
            ac.wait_ge(S["sqrt_v"], 1)
            ac.activation(rn, var, ACT.Sqrt, scale=float(D)).then_inc(S["sqrt_done"], 1)
            ac.wait_ge(S["gap_ready"], 1)
            ac.activation(pr, pr, ACT.Exp).then_inc(S["exp_gap"], 1)
            ac.activation(aneg[:, :], aneg[:, :], ACT.Exp).then_inc(S["aneg_exp"], 1)

            def take_u(c):
                ac.wait_ge(S["pr_tr"], c + 1)
                if c:
                    ac.wait_ge(S["pr_x"], c)
                    ac.wait_ge(S["pr_du"], KC * c)
                for k in range(KC):
                    ac.copy(ut[:, k, :], (fa[0], fb[0])[k][:, :]).then_inc(S["pr_ut"], 1)

            def prepare(c):
                ac.wait_ge(S["pr_x"], c + 1)
                if c:
                    ac.wait_ge(S["bc_put"], 16 * c)
                    ac.wait_ge(S["pr_dp"], KC * c)
                ac.copy(xd[0:NX, :], fa[1][0:NX, :]).then_inc(S["pr_xd"], 1)
                ac.wait_ge(S["pr_xd"], c + 1)
                ac.dma_start(bc_d[c], xd[DTR:NX, :]).then_inc(S["bc_put"], 16)
                for h in range(KC):
                    ac.wait_ge(S["pr_dp"], KC * c + h + 1)
                    if c:
                        ac.wait_ge(S["pr_de"], KC * (c - 1) + h + 1)
                    ac.activation(el[h], (fb[1], pt)[h][:, :], ACT.Abs).then_inc(S["pr_ab"], 1)
                for h in range(KC):
                    ac.wait_ge(S["pr_ab"], KC * c + h + 1)
                    ac.activation(el[h], el[h], ACT.Exp, scale=-1.0).then_inc(S["pr_ex"], 1)
                for h in range(KC):
                    ac.wait_ge(S["pr_ex"], KC * c + h + 1)
                    ac.activation(el[h], el[h], ACT.Ln, bias=1.0).then_inc(S["pr_ln"], 1)

            def exps(c, g):
                u = unit_index(c, g)
                ac.wait_ge(dd_in[g % 2], 64 * (c * (G // 2) + g // 2 + 1))
                if not (isinstance(c, int) and c == 0 and g < RING):
                    ac.wait_ge(S["sum_done"], u - RING + 1)
                for n in range(NH):
                    ins = ac.activation(ring[:, g % RING, n, :], dd[:, g % 2, 0, :], ACT.Exp,
                                        scale=aneg[:, NH * g + n:NH * g + n + 1])
                ins.then_inc(S["exp_done"], 1)

            def take_y(c, g, last=False):
                u = unit_index(c, g)
                ac.wait_ge(S["ytr_done"], u + 1)
                if not last:
                    ac.wait_ge(S["sum_done"], u + 2)
                if g == 0 and not (isinstance(c, int) and c == 0):
                    ac.wait_ge(S["yb_done"], c)
                ac.copy(ya[:, :, DG * g:DG * g + DG], py[:, 384:512].rearrange("p (j d) -> p j d", j=TPC)).then_inc(S["ya_done"], 1)

            def hand_over(c):
                ac.wait_ge(S["ya_done"], G * (c + 1))
                ac.wait_ge(S["yb_put"], 64 * c + 16)
                ac.copy(idb[:, :], ids[:, bass.ds(c * TPC, TPC)]).then_inc(S["idb_done"], 1)
                ac.wait_ge(S["idb_done"], c + 1)
                ac.copy(yb[:, :, :].rearrange("p t c -> p (t c)"), ya[:, :, :].rearrange("p t c -> p (t c)")).then_inc(S["yb_done"], 1)

            def take_sum(c, g):
                u = unit_index(c, g)
                ac.wait_ge(S["sum_done"], u + 1)
                if not (isinstance(c, int) and c == 0 and g == 0):
                    ac.wait_ge(S["ytr_done"], u)
                ac.copy(y1[:, :], py[:, 256:384]).then_inc(S["y1_done"], 1)

            take_u(0)
            prepare(0)
            ac.wait_ge(S["aneg_exp"], 2)
            ac.wait_ge(S["acc_put"], 16 * NCH)
            for k in range(G):
                if k + 1 < NCH:
                    take_u(k + 1)
                exps(0, k)
                if k >= 3:
                    take_y(0, k - 3)
                if k >= 2:
                    take_sum(0, k - 2)
                if k + 1 < NCH:
                    prepare(k + 1)

            def evac_xt(j, parity):
                ac.wait_ge(S["xtr_done"], j + 1)
                ac.copy(xt[:, parity, :], pt[:, 0:D]).then_inc(S["xt_done"], 1)

            def tanh(j, parity):
                ac.wait_ge(S["a_done"], j + 1)
                ac.activation(sg[:, parity, :], fa[parity][:, :], ACT.Tanh, scale=0.5).then_inc(S["tanh_done"], 1)

            def evac_ht(j):
                ac.wait_ge(S["htr_done"], j + 1)
                ac.copy(ht, pt[:, :]).then_inc(S["ht_done"], 1)

            def evac_y(j, parity, slot, before):
                ac.wait_ge(S["w2_done"], j + 1)
                ac.wait_ge(S[f"ye_put{parity}"], before)
                ac.activation(ye[:, parity, :], py[:, 0:D], ACT.Copy, scale=meta[:, slot, 1:2]).then_inc(S["ye_done"], 1)

            ac.sem_inc(S["ye_done"], 1)
            evac_xt(0, 0)
            tanh(0, 0)
            evac_xt(1, 1)
            with ac.Fori(0, TURNS) as i:
                c = i + 1
                for s in range(SPI):
                    j = SPI * i + 1 + s
                    k = UNIT_OF_STEP.get(s)
                    tanh(j, (s + 1) % 2)
                    evac_ht(j - 1)
                    if k is not None:
                        if k >= 3:
                            take_y(c, k - 3)
                        else:
                            take_y(i, k + G - 3)
                        if k >= 2:
                            take_sum(c, k - 2)
                        else:
                            take_sum(i, k + G - 2)
                    ac.wait_ge(S["b_done"], j)
                    evac_xt(j + 1, s % 2)
                    if k is not None:
                        exps(c, k)
                    if k == 2:
                        hand_over(i)
                    evac_y(j - 1, s % 2, s, 16 * (SPI // 2 * i + s // 2 + 1))
            evac_ht(FT - 1)
            evac_y(FT - 1, (FT - 1) % 2, (FT - 1) % SPI, 16 * ((FT - 1) // 2 + 1))
            c = NCH - 1
            take_y(c, G - 3)
            take_sum(c, G - 2)
            take_y(c, G - 2)
            take_sum(c, G - 1)
            take_y(c, G - 1, last=True)
            hand_over(c)

        @block.vector
        def _(ve):
            chained = [0]

            def link(ins, base=0):
                chained[0] += 1
                ins.then_inc(S["chain"], 1)
                ve.wait_ge(S["chain"], base + chained[0])

            ve.memset(pad[:, :, 0:D], 0.0).then_inc(S["pad_ready"], 1)
            ve.sem_inc(S["acc_ready"], 1)
            ve.memset(pad[:, :, D + 1:ROWW], 0.0).then_inc(S["pad_ready"], 1)
            ve.memset(ones, 1.0)
            ve.memset(one_row[:, :], 1.0)
            ve.memset(state[:, :], 0.0)
            ve.memset(cpT[:, :], 0.0)
            link(ve.memset(keep[:, :], 1.0))
            ve.memset(keep[:, CPB:CPB + 1], 0.0).then_inc(S["dve_const"], 1)
            ve.wait_ge(S["const_in"], 16 * 11)
            ve.tensor_tensor_reduce(mjunk, mnat, mnat, 1.0, 0.0, ALU.mult, ALU.add, msum).then_inc(S["norm_sq"], 1)
            ve.wait_ge(S["norm_sqrt"], 1)
            link(ve.tensor_scalar(mrec, mrec, EPS_NORM, None, ALU.max))
            link(ve.reciprocal(mrec, mrec))
            ve.tensor_scalar(mnrm, mnat, mrec, None, ALU.mult).then_inc(S["norm_ready"], 1)

            before_ln = chained[0]
            LN_LINKS = 16
            with ve.Fori(0, NCH // 2) as i:
                base = i * LN_LINKS
                for h in range(2):
                    q4 = 8 * i + 4 * h
                    x_t = [xin[:, bass.ds(q4 + t, 1), :].rearrange("p o d -> p (o d)") for t in range(TPC)]
                    ve.wait_ge(x_sem[h], 16 * (i + 1))
                    for t in range(TPC):
                        ins = ve.bn_stats(stats[:, t, :], x_t[t])
                    link(ins, base)
                    apart(ve)
                    for t in range(TPC):
                        ins = ve.bn_aggr(mv[:, t, :], stats[:, t, :])
                    link(ins, base)
                    ve.tensor_copy(var[:, bass.ds(q4, TPC)], mv[:, :, 1])
                    ve.tensor_scalar(rt, mv[:, :, 1], EPS_LN, None, ALU.add).then_inc(S["ln_stats"], 1)
                    ve.wait_ge(S["ln_stats"], 2 * i + h + 1)
                    ve.wait_ge(S["ln_sd"], 2 * i + h + 1)
                    link(ve.reciprocal(rs, sd), base)
                    link(ve.tensor_tensor(sd, rs, rs, ALU.mult), base)
                    link(ve.tensor_tensor(sd, sd, rt, ALU.mult), base)
                    link(ve.tensor_scalar(sd, sd, -0.5, 1.5, ALU.mult, ALU.add), base)
                    link(ve.tensor_tensor(rs, rs, sd, ALU.mult), base)
                    link(ve.tensor_copy(rstd[:, bass.ds(q4, TPC)], rs), base)
                    for t in range(TPC):
                        ve.tensor_scalar(row[:, bass.ds(q4 + t, 1), 0:D].rearrange("p o d -> p (o d)"), x_t[t],
                                         mv[:, t, 0:1], rs[:, t:t + 1], ALU.subtract, ALU.mult).then_inc(S["ln_rows"], 1)
            assert chained[0] - before_ln == LN_LINKS
            chained[0] = before_ln + LN_LINKS * (NCH // 2)
            ve.wait_ge(S["ln_rows"], NT)
            ve.engine_nop().then_inc(S["sqrt_v"], 1)

            def over_k(v):
                return v.rearrange("p (t o) -> p t o", o=1).to_broadcast([P, NT, NB])

            def over_t(v):
                return v.rearrange("p (o k) -> p o k", o=1).to_broadcast([P, NT, NB])

            def first_largest(src, top, onehot):
                link(ve.tensor_reduce(top, src, AX, ALU.max))
                link(ve.tensor_tensor(eq, src, over_k(top), ALU.is_equal))
                link(ve.tensor_tensor(eq, eq, over_t(km8), ALU.mult))
                link(ve.tensor_reduce(mn8, eq, AX, ALU.min))
                link(ve.tensor_tensor(onehot, over_t(km8), over_k(mn8), ALU.is_equal))

            ve.wait_ge(S["ln_mm"], NCH + 2)
            ve.wait_ge(S["pool_const"], 7)
            link(ve.tensor_copy(lg.rearrange("p t c -> p (t c)"), py[:, :]))
            first_largest(lg[:, :, NB:2 * NB], m1, o1)
            link(ve.scalar_tensor_tensor(l2, o1, -BIG, lg[:, :, NB:2 * NB], ALU.mult, ALU.add))
            first_largest(l2, m2, o2)
            ve.tensor_tensor(pr, m2, m1, ALU.subtract).then_inc(S["gap_ready"], 1)
            link(ve.tensor_tensor(mk[:, 1, :, :], o1, o2, ALU.add))
            ve.wait_ge(S["sqrt_done"], 1)
            link(ve.tensor_tensor(rn, rn, rstd, ALU.mult))
            link(ve.tensor_scalar(rn, rn, EPS_NORM, None, ALU.max))
            link(ve.reciprocal(rn, rn))
            link(ve.tensor_tensor(sc, lg[:, :, 0:NB], over_k(rn), ALU.mult))
            first_largest(sc, mx, mk[:, 0, :, :])
            ve.engine_nop().then_inc(S["masks_ready"], 1)
            ve.wait_ge(S["exp_gap"], 1)
            link(ve.tensor_scalar(mx, pr, 1.0, None, ALU.add))
            link(ve.reciprocal(mx, mx))
            ve.tensor_copy(row[:, :, D + 1], mx).then_inc(S["probs_ready"], 1)
            ve.tensor_tensor(prob2[:, :], pr, mx, ALU.mult).then_inc(S["probs_ready"], 1)

            half = NT * NB
            ranks, totals = pb[:, 0:2 * half], pb[:, 2 * half:4 * half]
            by_i = dict(b=BATCH, k=NB)

            def tiles_last(v, kind):
                return v[:, 0:half].rearrange("p (b k i) -> p b k i", **by_i) if kind == 0 else \
                    v[:, half:2 * half].rearrange("p (k i) -> p k i", k=NB)

            ve.wait_ge(S["ranks_ready"], 1)
            ve.tensor_copy(tiles_last(cn, 0), totals[:, 0:half].rearrange("p (b i k) -> p b k i", **by_i))
            link(ve.tensor_copy(tiles_last(cn, 1), totals[:, half:2 * half].rearrange("p (i k) -> p k i", k=NB)))
            for a in (0, half):
                ins = ve.tensor_tensor_scan(cs[:, a:a + half], ones[:, 0:half], cn[:, a:a + half], 0.0, ALU.mult, ALU.add)
            link(ins)
            link(ve.tensor_tensor(ex, cs, cn, ALU.subtract))
            link(ve.tensor_tensor(adr[:, 0, :, :].rearrange("p (b i) k -> p b i k", b=BATCH),
                                  ranks[:, 0:half].rearrange("p (b i k) -> p b i k", **by_i),
                                  ex[:, 0:half].rearrange("p (b k i) -> p b i k", **by_i), ALU.add))
            link(ve.tensor_tensor(adr[:, 0, :, :], adr[:, 0, :, :], mk[:, 0, :, :], ALU.mult))
            link(ve.tensor_reduce(posf, adr[:, 0, :, :], AX, ALU.add))
            ve.tensor_copy(pos_a[:, :], posf).then_inc(S["pos_ready"], 1)
            start = tiles_last(ex, 1)[:, :, 0]
            link(ve.tensor_tensor(tl, tiles_last(cs, 1)[:, :, NT - 1], start, ALU.subtract))
            link(ve.tensor_scalar(tli.bitcast(I32), tl, float(P - 1), None, ALU.add))
            link(ve.tensor_scalar(tli.bitcast(I32), tli.bitcast(I32), P.bit_length() - 1, None, ALU.arith_shift_right))
            link(ve.tensor_copy(tl, tli.bitcast(I32)))
            link(ve.tensor_tensor_scan(ct, ones[:, 0:NB], tl, 0.0, ALU.mult, ALU.add))
            link(ve.tensor_tensor(off, ct, tl, ALU.subtract))
            link(ve.scalar_tensor_tensor(off, off, float(P), start, ALU.mult, ALU.subtract))
            link(ve.tensor_tensor(tiles_last(ex, 1), tiles_last(ex, 1),
                                  off.rearrange("p (k o) -> p k o", o=1).to_broadcast([P, NB, NT]), ALU.add))
            link(ve.tensor_tensor(adr[:, 1, :, :], ranks[:, half:2 * half].rearrange("p (i k) -> p i k", k=NB),
                                  ex[:, half:2 * half].rearrange("p (k i) -> p i k", k=NB), ALU.add))
            for onehot, pos in ((o1, pos_1), (o2, pos_2)):
                link(ve.tensor_tensor(eq, adr[:, 1, :, :], onehot, ALU.mult))
                link(ve.tensor_reduce(posf, eq, AX, ALU.add))
                link(ve.tensor_copy(pos[:, :], posf))
            ve.engine_nop().then_inc(S["ffn_pos_ready"], 1)
            last = NB - 1
            link(ve.tensor_tensor(ge[:, :, 0:last], jt.rearrange("p (j o) -> p j o", o=1).to_broadcast([1, FTP, last]),
                                  ct[0:1, 0:last].rearrange("p (o k) -> p o k", o=1).to_broadcast([1, FTP, last]), ALU.is_ge))
            link(ve.tensor_reduce(etf, ge[:, :, 0:last], AX, ALU.add))
            link(ve.tensor_copy(etab[:, :], etf))
            diag = ident[0:NB, 0:NB].rearrange("p (o k) -> p o k", o=1).to_broadcast([NB, BATCH, NB])
            for src, at, one, per_chunk in ((ex, 0, lo1, lo_c), (cs, NT // BATCH - 1, hi1, hi_c)):
                link(ve.tensor_tensor(lo2, src[0:NB, 0:half].rearrange("p (b k i) -> p b k i", **by_i)[:, :, :, at], diag, ALU.mult))
                link(ve.tensor_reduce(one, lo2, AX, ALU.add))
                link(ve.tensor_tensor(per_chunk[:, :].rearrange("p (b c) -> p b c", b=BATCH),
                                      one.rearrange("p (b o) -> p b o", o=1).to_broadcast([NB, BATCH, CPB]),
                                      c512.rearrange("p (b c) -> p b c", b=BATCH), ALU.subtract))

            before_acc = chained[0]
            with ve.Fori(0, NCH) as q:
                x_q = xin[:, bass.ds(TPC * q, TPC), :]
                ve.wait_ge(S["acc_ready"], q + 1)
                link(ve.tensor_tensor(skip, row[:, bass.ds(TPC * q, TPC), 0:D],
                                      dsb.rearrange("p (o d) -> p o d", o=1).to_broadcast([P, TPC, D]), ALU.mult), q)
                ve.tensor_tensor(x_q, x_q, skip, ALU.add).then_inc(S["acc_ready"], 1)
            assert chained[0] - before_acc == 1
            chained[0] = before_acc + NCH
            ve.wait_ge(S["aneg_exp"], 1)
            ve.tensor_scalar(aneg[:, :], aneg[:, :], -1.0, None, ALU.mult).then_inc(S["aneg_exp"], 1)

            def cluster_rows(c):
                if c:
                    ve.wait_ge(S["pr_x"], c)
                link(ve.tensor_scalar(over, iota512[:, :], hi_c[:, c:c + 1], None, ALU.is_ge))
                ve.scalar_tensor_tensor(osort, iota512[:, :], lo_c[:, c:c + 1], over, ALU.is_ge, ALU.subtract).then_inc(S["pr_os"], 1)

            def prepare(c):
                ve.wait_ge(S["xs_in"], 16 * (c + 1))
                ve.tensor_copy(ids[:, TPC * c:TPC * c + TPC], xsr.bitcast(U32)[:, :, D]).then_inc(S["pr_ids"], 1)
                for h in range(KC):
                    n = KC * c + h
                    ve.wait_ge(S["pr_ln"], n + 1)
                    if c:
                        ve.wait_ge(S[f"dd_put{h}"], 16 * c)
                    ve.scalar_tensor_tensor(ddst[h][:, 0, :], (fb[1], pt)[h][:, :], 0.0, el[h], ALU.max, ALU.add).then_inc(S["pr_de"], 1)
                    ve.wait_ge(S["pr_de"], n + 1)
                    ve.wait_ge(S["pr_ut"], KC * (c + 1))
                    ve.tensor_tensor(ddst[h][:, 1, :], ddst[h][:, 0, :], ut[:, h, :], ALU.mult).then_inc(S["pr_du"], 1)

            def unit(c, g, parity):
                u = unit_index(c, g)
                ve.wait_ge(dd_in[g % 2], 64 * (c * (G // 2) + g // 2 + 1))
                for half2 in range(2):
                    b_rows = bc[:, parity, 0, 2 * half2:2 * half2 + 2, :] if isinstance(parity, int) else \
                        bc[:, bass.ds(parity, 1), 0, 2 * half2:2 * half2 + 2, :].rearrange("p o n c -> p (o n) c")
                    if not (isinstance(c, int) and c == 0 and g == 0 and half2 == 0):
                        ve.wait_ge(S["scan_done"], 4 * u + 2 * half2)
                    ve.tensor_tensor(pb[:, :].rearrange("p (n c) -> p n c", n=2),
                                     dd[:, g % 2, 1, :].rearrange("p (o c) -> p o c", o=1).to_broadcast([P, 2, CH]),
                                     b_rows, ALU.mult).then_inc(S["dbu_done"], 1)
                    ve.wait_ge(S["dbu_done"], 2 * u + half2 + 1)
                    if half2 == 0:
                        ve.wait_ge(S["exp_done"], u + 1)
                    for m in range(2):
                        n = 2 * half2 + m
                        r = ring[:, g % RING, n, :]
                        ve.tensor_tensor_scan(r, r, pb[:, CH * m:CH * m + CH], state[:, NH * g + n:NH * g + n + 1],
                                              ALU.mult, ALU.add).then_inc(S["scan_done"], 1)
                ve.wait_ge(S["scan_done"], 4 * u + 4)
                ve.tensor_copy(state[:, NH * g:NH * g + NH], ring[:, g % RING, :, CH - 1]).then_inc(S["h_ready"], 1)

            cluster_rows(0)
            prepare(0)
            ve.wait_ge(S["bc_in"], 128)
            ve.wait_ge(S["aneg_exp"], 2)
            for k in range(G):
                if k + 1 < NCH:
                    cluster_rows(k + 1)
                unit(0, k, 0)
                r = ring[:, k % RING, :, :].rearrange("p n c -> p (n c)")
                ve.wait_ge(S["h_ready"], k + 1)
                ve.tensor_tensor(r, r, bc[:, 0, 1, :, :].rearrange("p n c -> p (n c)"), ALU.mult).then_inc(S["hc_done"], 1)
                if k + 1 < NCH:
                    prepare(k + 1)

            def silu(j, parity):
                ve.wait_ge(S["tanh_done"], j + 1)
                s = sg[:, parity, :]
                ve.scalar_tensor_tensor(s, s, 1.0, fa[parity][:, :], ALU.add, ALU.mult).then_inc(S["s1_done"], 1)
                ve.wait_ge(S["s1_done"], j + 1)
                ve.wait_ge(S["b_done"], j + 1)
                ve.scalar_tensor_tensor(s, s, 0.5, fb[parity][:, :], ALU.mult, ALU.mult).then_inc(S["silu_done"], 1)

            silu(0, 0)
            with ve.Fori(0, TURNS) as i:
                c = i + 1
                ve.wait_ge(S["h_ready"], G * c)
                ve.tensor_scalar(state[:, :], state[:, :], keep[:, bass.ds(c, 1)], None, ALU.mult).then_inc(S["keep_done"], 1)
                ve.wait_ge(S["keep_done"], c)
                ve.wait_ge(S["bc_in"], 128 * (c + 1))
                for s in range(SPI):
                    silu(SPI * i + 1 + s, (s + 1) % 2)
                    k = UNIT_OF_STEP.get(s)
                    if k is not None:
                        unit(c, k, (i + 1) % 2)
            for q in range(NCH):
                a, b1, b2 = [w[:, TPC * D * q:TPC * D * q + TPC * D] for w in (w1, w3, w2)]
                ve.wait_ge(S[f"parts_in{q}"], 48)
                ve.tensor_tensor(a, a, b1, ALU.add).then_inc(S["out_ready"], 1)
                ve.wait_ge(S["out_ready"], 2 * q + 1)
                ve.tensor_tensor(a, a, b2, ALU.add).then_inc(S["out_ready"], 1)

        @block.tensor
        def _(pe):
            pe.wait_ge(S["const_in"], 16 * 11)
            pe.wait_ge(S["pool_const"], 1)
            pe.wait_ge(S["norm_ready"], 1)
            for k in range(KC):
                cols = slice(P * k, P * k + P)
                pe.transpose(pt[:, NX * k:NX * k + NX], xpnat[:, cols], ident[0:NX, 0:NX])
                pe.transpose(pt[:, 128 + NB * k:136 + NB * k], mnrm[:, cols], ident[0:NB, 0:NB])
                pe.transpose(pt[:, 144 + NB * k:152 + NB * k], mnat[:, cols], ident[0:NB, 0:NB])
                pe.transpose(pt[:, 160 + NS * k:176 + NS * k], pnat[:, cols], ident[0:NS, 0:NS])
                ins = pe.transpose(pt[0:DTR, 192 + P * k:192 + P * k + P], dtnat[:, k, :], ident[:, :])
            ins.then_inc(S["small_tr"], 1)
            pe.wait_ge(S["small_cp"], 5)
            for k in range(KC):
                ins = pe.matmul(py[0:NB, 0:NS], mT[:, k, :], pT[:, k, :], start=(k == 0), stop=(k == KC - 1))
            ins.then_inc(S["ln_mm"], 2)
            pe.wait_ge(S["cp_ready"], 1)
            def turn_tokens(q):
                h = q % 2
                if q > 1:
                    pe.wait_ge(S["ln_ev"], 2 * (q - 1))
                for t in range(TPC):
                    pe.wait_ge(S["ln_rows"], TPC * q + t + 1)
                    for k, dst in enumerate((fa[h], fb[h])):
                        ins = pe.transpose(dst[:, P * t:P * t + P], row[:, TPC * q + t, P * k:P * k + P], ident[:, :])
                ins.then_inc(S["ln_tr"], 1)

            turn_tokens(0)
            for q in range(NCH):
                if q + 1 < NCH:
                    turn_tokens(q + 1)
                pe.wait_ge(S["ln_ev"], 2 * (q + 1))
                for t in range(TPC):
                    col = 16 * (TPC * q + t)
                    for k in range(KC):
                        ins = pe.matmul(py[:, col:col + 16], xnT[:, q % 2, k, P * t:P * t + P], wg[:, k, :],
                                        start=(k == 0), stop=(k == KC - 1))
                ins.then_inc(S["ln_mm"], 1)
            pe.wait_ge(S["masks_ready"], 1)
            pe.wait_ge(S["pool_const"], 2)
            masks = mk.rearrange("p a t k -> p (a t k)")
            pe.matmul(pb[:, 0:512], tri, masks, start=True, stop=True)
            pe.matmul(pb[:, 512:1024], ones[:, 0:P], masks, start=True, stop=True).then_inc(S["ranks_ready"], 1)

            def turn_rows(c):
                pe.wait_ge(S["xs_in"], 16 * (c + 1))
                pe.wait_ge(S["pr_ut"], KC * c) if c else pe.wait_ge(S["ln_ev"], 2 * NCH)
                for t in range(TPC):
                    for k in range(KC):
                        ins = pe.transpose((fa[0], fb[0])[k][:, P * t:P * t + P], xsr[:, t, P * k:P * k + P], ident[:, :])
                ins.then_inc(S["pr_tr"], 1)

            def prepare(c):
                pe.wait_ge(S["pr_ut"], KC * (c + 1))
                pe.wait_ge(S["pr_os"], c + 1)
                if c:
                    pe.wait_ge(S["pr_xd"], c)
                for k in range(KC):
                    pe.matmul(fa[1][0:NX, :], xprojT[:, k, :], ut[:, k, :], start=(k == 0), stop=False)
                pe.matmul(fa[1][0:NX, :], cpT[:, :], osort, start=False, stop=True).then_inc(S["pr_x"], 1)
                pe.wait_ge(S["pr_xd"], c + 1)
                for h in range(KC):
                    if c:
                        pe.wait_ge(S["pr_de"], KC * (c - 1) + h + 1)
                    dst = (fb[1], pt)[h]
                    pe.matmul(dst[:, :], dtwT[:, P * h:P * h + P], xd[0:DTR, :], start=True, stop=False)
                    pe.matmul(dst[:, :], dtb[:, P * h:P * h + P], one_row[:, :], start=False, stop=True).then_inc(S["pr_dp"], 1)

            def fold_states(c, g):
                u = unit_index(c, g)
                pe.wait_ge(S["hc_done"], u + 1)
                if not (isinstance(c, int) and c == 0 and g == 0):
                    pe.wait_ge(S["y1_done"], u)
                for n in range(NH):
                    for q in range(TPC):
                        ins = pe.matmul(py[DG * q:DG * q + DG, 256:384], fold[:, :], ring[:, g % RING, n, P * q:P * q + P],
                                        start=(n == 0), stop=(n == NH - 1), tile_position=(0, DG * q))
                ins.then_inc(S["sum_done"], 1)

            def turn_y(c, g):
                u = unit_index(c, g)
                pe.wait_ge(S["y1_done"], u + 1)
                if not (isinstance(c, int) and c == 0 and g == 0):
                    pe.wait_ge(S["ya_done"], u)
                pe.transpose(py[:, 384:512], y1[:, :], ident[:, :]).then_inc(S["ytr_done"], 1)

            turn_rows(0)
            prepare(0)
            for k in range(G):
                if k + 1 < NCH:
                    turn_rows(k + 1)
                if k >= 3:
                    turn_y(0, k - 3)
                if k >= 2:
                    fold_states(0, k - 2)
                if k + 1 < NCH:
                    prepare(k + 1)

            def turn_x(j, parity, landed):
                pe.wait_ge(xr_in[parity], landed)
                for k in range(KC):
                    ins = pe.transpose(pt[:, P * k:P * k + P], xr[:, parity, P * k:P * k + P], ident[:, :])
                ins.then_inc(S["xtr_done"], 1)

            def expert_of(j):
                apart(pe)
                return pe.value_load(etab[0:1, bass.ds(j, 1)], min_val=0, max_val=E - 1)

            def up(j, parity, e):
                pe.wait_ge(S["xt_done"], j + 1)
                for w, dst, done in ((w1, fa[parity], S["a_done"]), (w3, fb[parity], S["b_done"])):
                    for k in range(KC):
                        ins = pe.matmul(dst[:, :], xt[:, parity, P * k:P * k + P],
                                        w[:, bass.ds(e * (KC * H) + H * k, H)], start=(k == 0), stop=(k == KC - 1))
                    ins.then_inc(done, 1)

            def turn_h(j, parity):
                pe.wait_ge(S["silu_done"], j + 1)
                for k in range(HC):
                    ins = pe.transpose(pt[:, P * k:P * k + P], sg[:, parity, P * k:P * k + P], ident[:, :])
                ins.then_inc(S["htr_done"], 1)

            def down(j, e):
                pe.wait_ge(S["ht_done"], j + 1)
                for k in range(HC):
                    ins = pe.matmul(py[:, 0:D], ht[:, P * k:P * k + P],
                                    w2[:, bass.ds(e * (HC * D) + D * k, D)], start=(k == 0), stop=(k == HC - 1))
                ins.then_inc(S["w2_done"], 1)

            pe.wait_ge(S["pr_de"], KC * NCH)
            pe.wait_ge(S["pr_xd"], NCH)
            pe.wait_ge(S["w13_in"], 16 * 2 * E)
            turn_x(0, 0, 32)
            up(0, 0, expert_of(0))
            turn_x(1, 1, 32)
            pe.wait_ge(S["w2_in"], 16 * E)
            with pe.Fori(0, TURNS) as i:
                c = i + 1
                for s in range(SPI):
                    j = SPI * i + 1 + s
                    k = UNIT_OF_STEP.get(s)
                    e_up, e_down = expert_of(j), expert_of(j - 1)
                    up(j, (s + 1) % 2, e_up)
                    turn_h(j - 1, s % 2)
                    pe.wait_ge(S["ye_done"], j)
                    if k is not None:
                        if k >= 3:
                            turn_y(c, k - 3)
                        else:
                            turn_y(i, k + G - 3)
                        if k >= 2:
                            fold_states(c, k - 2)
                        else:
                            fold_states(i, k + G - 2)
                    pe.wait_ge(S["ht_done"], j)
                    turn_x(j + 1, s % 2, 32 * (SPI // 2 * i + (s + 2) // 2 + 1))
                    if k is not None:
                        pe.wait_ge(S["ya_done"], unit_index(c, k) - 2)
                        pe.wait_ge(S["y1_done"], unit_index(c, k) - 1)
                    down(j - 1, e_down)
            pe.wait_ge(S["xt_done"], FT + 1)
            e_last = expert_of(FT - 1)
            turn_h(FT - 1, (FT - 1) % 2)
            pe.wait_ge(S["ye_done"], FT)
            down(FT - 1, e_last)
            c = NCH - 1
            pe.wait_ge(S["ye_done"], FT + 1)
            turn_y(c, G - 3)
            fold_states(c, G - 2)
            turn_y(c, G - 2)
            fold_states(c, G - 1)
            turn_y(c, G - 1)


_INS = ["L0_attn_x", "L0_attn_means", "L0_attn_prompt_weight", "L0_attn_x_proj_weight", "L0_attn_dt_projs_weight",
        "L0_attn_dt_projs_bias", "L0_attn_A_logs", "L0_attn_Ds", "L0_ffn_w_gate", "L0_ffn_w1", "L0_ffn_w3", "L0_ffn_w2"]
_OUTS = [((BATCH, LEN, D), "float32")]


def kernel(**inputs):
    import numpy as _np
    import concourse.bacc as _bacc
    from concourse import mybir as _mybir
    from concourse.bass_utils import run_bass_kernel_spmd as _run

    nc = _bacc.Bacc("TRN2", target_bir_lowering=False, num_devices=1)
    arrays, args = {}, []
    for name in _INS:
        a = _np.ascontiguousarray(inputs[name])
        arrays[f"in_{name}_dram"] = a
        args.append(nc.dram_tensor(f"in_{name}_dram", a.shape, _mybir.dt.from_np(a.dtype), kind="ExternalInput").ap())
    for i, (shape, dtype) in enumerate(_OUTS):
        dt = _mybir.dt.from_np(_np.dtype(dtype))
        args.append(nc.dram_tensor(f"out_{i}_dram", shape, dt, kind="ExternalOutput").ap())
    program(nc, *args)
    r = _run(nc, [arrays], core_ids=[0])
    got = tuple(r.results[0][f"out_{i}_dram"] for i in range(len(_OUTS)))
    return got[0]
```

```python
from contextlib import ExitStack

import concourse.bass as bass
from concourse import mybir

F32 = mybir.dt.float32
U32 = mybir.dt.uint32
I32 = mybir.dt.int32
ALU = mybir.AluOpType
ACT = mybir.ActivationFunctionType
AX = mybir.AxisListType.X

P = 128
BATCH, LEN, D = 2, 2048, 256
TOK = BATCH * LEN
NT = TOK // P
KC = D // P
NB = 8
NS, DTR = 16, 32
NX = DTR + 2 * NS
E, H = 8, 512
HC = H // P
ROWW = D + 2
FT = (2 * TOK) // P + E - 1
FTP = FT + 1
CH = 512
NCH = TOK // CH
CPB = LEN // CH
TPC = CH // P
DG = 32
G = D // DG
NH = 4
RING = 4
SPI = G
REST = range(SPI * NCH + 1, FT)
CONST_LOADS = 12
EPS_LN, EPS_NORM = 1e-5, 1e-12
BIG = 3.0e38


def program(nc, x_in, means_in, prompt_in, xproj_in, dtw_in, dtb_in, alog_in, ds_in, gate_in, w1_in, w3_in, w2_in, out):
    with ExitStack() as ctx:
        def sb(name, shape, dt=F32):
            return ctx.enter_context(nc.sbuf_tensor(name, shape, dt))

        def sem(name):
            return ctx.enter_context(nc.semaphore(name))

        def dram(name, shape):
            return nc.dram_tensor(name, shape, F32, kind="Internal").ap()

        xs_d = dram("xs_d", [TOK, D + 1])
        xe_d = dram("xe_d", [FTP * P, ROWW])
        bc_d = dram("bc_d", [NCH, 2 * NS, CH])
        dd_d = dram("dd_d", [NCH * D, 2 * CH])
        acc_d = dram("acc_d", [TOK, D])
        y_d = dram("y_d", [TOK + P, D])

        ring = sb("ring", [P, RING, NH, CH])
        bc = sb("bc", [P, 2, 2, NH, CH])
        late = sb("late", [P, 2 * 2 * CH + 2 * TPC * D])
        dd = late[:, 0:2048].rearrange("p (s r c) -> p s r c", s=2, r=2)
        w1 = sb("w1", [P, E * KC * H])
        w3 = sb("w3", [P, E * KC * H])
        w2x = sb("w2x", [P, NT * ROWW])
        w2 = w2x[:, 0:E * HC * D]
        row = w2x[:, :].rearrange("p (t c) -> p t c", c=ROWW)
        row_u = row.bitcast(U32)
        ya = late[:, 2048:3072].rearrange("p (t c) -> p t c", t=TPC)
        yb = late[:, 3072:4096].rearrange("p (t c) -> p t c", t=TPC)
        idb = sb("idb", [P, TPC], U32)
        ids = sb("ids", [P, NT], U32)
        state = sb("state", [P, G * NH])
        keep = sb("keep", [P, NCH])
        aneg = sb("aneg", [P, G * NH])
        ident = sb("ident", [P, P])
        fold = sb("fold", [P, DG])
        y1 = sb("y1", [P, P])
        meta = sb("meta", [P, SPI, 2])
        etab = sb("etab", [1, FTP], I32)

        pool = sb("pool", [P, 5128])
        xr = pool[:, 0:512].rearrange("p (s c) -> p s c", s=2)
        xt = pool[:, 512:1024].rearrange("p (s c) -> p s c", s=2)
        sg = pool[:, 1024:2048].rearrange("p (s c) -> p s c", s=2)
        ht = pool[:, 2048:2560]
        ye = pool[:, 2560:3072].rearrange("p (s c) -> p s c", s=2)
        flat = ring[:, :, :, :].rearrange("p a b c -> p (a b c)")

        def prep_buffers(v, el1, osort):
            return dict(xsr=v[:, 0:TPC * (D + 1)].rearrange("p (t c) -> p t c", c=D + 1),
                        xd=v[:, 2056:2568], el=[v[:, 2568:3080], el1],
                        dd=[v[:, 3080 + 1024 * h:4104 + 1024 * h].rearrange("p (k c) -> p k c", k=2) for h in range(KC)],
                        osort=osort)

        osort = [sb("osort0", [NB, CH])[:, :], sb("osort1", [NB, CH])[:, :]]
        prep = [prep_buffers(pool, late[:, 3072:3584], osort[0]),
                prep_buffers(flat, flat[:, 5128:5640], osort[1])]
        ut = [v.rearrange("p (k c) -> p k c", k=KC) for v in (pool[:, 1032:2056], flat[:, 1032:2056], flat[:, 6144:7168])]
        over = late[0:NB, 3584:4096]
        iota512 = sb("iota512", [NB, CH])

        xprojT = sb("xprojT", [P, KC, NX])
        dtwT = sb("dtwT", [DTR, D])
        dtb = sb("dtb", [P, KC])
        cpT = sb("cpT", [NB, NX])
        lo_c = sb("lo_c", [NB, NCH])
        hi_c = sb("hi_c", [NB, NCH])
        prob2 = sb("prob2", [P, NT])
        pos_a = sb("pos_a", [P, NT], U32)
        pos_1 = sb("pos_1", [P, NT], U32)
        pos_2 = sb("pos_2", [P, NT], U32)

        xin = ring[:, :, :, :].rearrange("p a b c -> p (a b c)").rearrange("p (t c) -> p t c", c=D)
        tmp = bc[:, :, :, :, :].rearrange("p a b c d -> p (a b c d)")
        room = [[tmp, 0, 2 * 2 * NH * CH], [late, 0, 4096]]

        def cut(n, parts=P):
            r = room[0] if room[0][1] + n <= room[0][2] else room[1]
            a = r[1]
            r[1] += n
            assert r[1] <= r[2]
            return r[0][0:parts, a:a + n]

        xnT = cut(2 * KC * CH).rearrange("p (s k c) -> p s k c", s=2, k=KC)
        lg = cut(NT * 16).rearrange("p (t c) -> p t c", c=16)
        pad = cut(ROWW)
        dsb = cut(D)
        ones = cut(2 * NB * NT)
        tri = cut(P)
        wg = cut(KC * 16).rearrange("p (k c) -> p k c", k=KC)
        nat = cut(D * 3 + 64)
        stats = cut(TPC * 6).rearrange("p (t c) -> p t c", c=6)
        mv = cut(TPC * 2).rearrange("p (t c) -> p t c", c=2)
        sd = cut(TPC)
        rs = cut(TPC)
        rt = cut(TPC)
        var = cut(NT)
        rstd = cut(NT)
        rn = cut(NT)
        km8 = cut(NB)
        mk = cut(2 * NT * NB).rearrange("p (a t k) -> p a t k", a=2, k=NB)
        o1 = cut(NT * NB).rearrange("p (t k) -> p t k", k=NB)
        o2 = cut(NT * NB).rearrange("p (t k) -> p t k", k=NB)
        sc = cut(NT * NB).rearrange("p (t k) -> p t k", k=NB)
        l2 = cut(NT * NB).rearrange("p (t k) -> p t k", k=NB)
        eq = cut(NT * NB).rearrange("p (t k) -> p t k", k=NB)
        mx = cut(NT)
        m1 = cut(NT)
        m2 = cut(NT)
        mn8 = cut(NT)
        pr = cut(NT)
        cn = cut(2 * NT * NB)
        cs = cut(2 * NT * NB)
        ex = cut(2 * NT * NB)
        adr = cut(2 * NT * NB).rearrange("p (a t k) -> p a t k", a=2, k=NB)
        tl = cut(NB)
        ct = cut(NB)
        off = cut(NB)
        tli = cut(NB)
        posf = cut(NT)
        jt = cut(FTP, 1)
        ge = cut(FTP * NB, 1).rearrange("p (j k) -> p j k", k=NB)
        etf = cut(FTP, 1)
        lo2 = cut(BATCH * NB, NB).rearrange("p (b k) -> p b k", b=BATCH)
        lo1 = cut(BATCH, NB)
        hi1 = cut(BATCH, NB)
        c512 = cut(NCH, NB)
        mnat = nat[0:NB, 0:D]
        mnrm = nat[0:NB, D:2 * D]
        mjunk = nat[0:NB, 2 * D:3 * D]
        msum = nat[0:NB, 3 * D:3 * D + 1]
        mrec = nat[0:NB, 3 * D + 1:3 * D + 2]
        pnat = cut(D, NS)
        xpnat = cut(D, NX)
        dtnat = cut(KC * DTR).rearrange("p (k r) -> p k r", k=KC)
        mT = cut(KC * NB).rearrange("p (k r) -> p k r", k=KC)
        pT = cut(KC * NS).rearrange("p (k r) -> p k r", k=KC)
        skip = pool[:, 5128 - TPC * D:5128].rearrange("p (t c) -> p t c", c=D)

        def ps(name, cols):
            return ctx.enter_context(nc.psum_tensor(name, [P, cols], F32))

        pb = ps("pb", 1024)
        fa = [ps("fa0", 512), ps("fa1", 512)]
        fb = [ps("fb0", 512), ps("fb1", 512)]
        pz = fb[1]
        pt = ps("pt", 512)
        py = ps("py", 512)
        rows_ps = [(fa[0][:, :], fb[0][:, :]), (pb[:, 0:512], pb[:, 512:1024])]
        x_ps = [fa[1], py]
        delta_ps = [fb[1], pt]

        names = """passed x_in0 x_in1 const_in pad_ready pad_put w13_in w2_in ln_stats ln_sd ln_rows ln_tr ln_ev
        ln_mm acc_ready acc_put pool_const dve_const small_tr small_cp cp_ready norm_sq norm_sqrt
        norm_ready sqrt_v sqrt_done chain masks_ready ranks_ready gap_ready exp_gap probs_ready pos_ready
        ffn_pos_ready pool_step xs_put0 xs_put1 xe_put1 xe_put2 aneg_exp
        xs_in0 xs_in1 pr_tr pr_ut pr_os pr_x pr_xd pr_dp pr_ab pr_ex pr_ln pr_de pr_du bc_put0 bc_put1 dd_put00 dd_put01 dd_put10 dd_put11 pr_ids pr_re
        bc_in dd_in0 dd_in1 exp_done dbu_done scan_done keep_done h_ready hc_done sum_done y1_done ytr_done
        ya_done yb_done idb_done
        xr_in0 xr_in1 xtr_done xt_done a_done b_done tanh_done s1_done silu_done htr_done ht_done w2_done ye_done
        out_ready out_put ye_put yb_put parts_in0 parts_in1 parts_in2 parts_in3 parts_in4 parts_in5 parts_in6
        parts_in7""".split()
        S = {n: sem(n) for n in names}
        x_sem = [S["x_in0"], S["x_in1"]]
        dd_in = [S["dd_in0"], S["dd_in1"]]
        xr_in = [S["xr_in0"], S["xr_in1"]]

        block = ctx.enter_context(nc.Block())

        def apart(eng):
            eng.sem_inc(S["passed"], 1)

        def unit_index(chunk, g):
            return chunk * G + g

        @block.sync
        def _(sp):
            x_v = x_in.rearrange("b (q j p) d -> (b q) p j d", p=P, j=TPC)
            for h in range(2):
                sp.dma_start(xin[:, TPC * h:TPC * h + TPC, :], x_v[h]).then_inc(x_sem[h], 16)
            with sp.Fori(1, NCH // 2) as i:
                for h in range(2):
                    sp.wait_ge(x_sem[h], 16 * i)
                    apart(sp)
                    sp.dma_start(xin[:, bass.ds(8 * i + 4 * h, TPC), :],
                                 x_v[bass.ds(2 * i + h, 1), :, :, :].rearrange("o p j d -> (o p) j d")).then_inc(x_sem[h], 16)
            sp.wait_ge(S["pad_ready"], 3)
            sp.dma_start(xe_d.rearrange("(t p) c -> p t c", p=P),
                         pad.rearrange("p (o c) -> p o c", o=1).to_broadcast([P, FTP, ROWW])).then_inc(S["pad_put"], 16)
            sp.dma_start(y_d[0:TOK, :].rearrange("(t p) c -> p t c", p=P),
                         pad[:, 0:D].rearrange("p (o c) -> p o c", o=1).to_broadcast([P, NT, D])).then_inc(S["pad_put"], 16)
            with sp.Fori(0, E) as e:
                for w, src in ((w1, w1_in), (w3, w3_in)):
                    sp.dma_start(w[:, bass.ds(e * (KC * H), KC * H)].rearrange("p (k h) -> p k h", k=KC),
                                 src[bass.ds(e, 1), :, :].rearrange("o (k p) h -> (o p) k h", p=P)).then_inc(S["w13_in"], 16)
            xs_v = xs_d.rearrange("(q j p) c -> q p j c", p=P, j=TPC)

            def load_sorted(c):
                sp.wait_ge(S[f"xs_put{c // CPB}"], 16 * NT // BATCH)
                if c >= 2:
                    sp.wait_ge(S["pr_tr"], c - 1)
                    sp.wait_ge(S["pr_ids"], c - 1)
                sp.dma_start(prep[c % 2]["xsr"], xs_v[c]).then_inc(S[f"xs_in{c % 2}"], 16)

            load_sorted(0)
            acc_v = acc_d.rearrange("(q j p) d -> q p j d", p=P, j=TPC)
            for q in range(NCH):
                sp.wait_ge(S["acc_ready"], q + 2)
                sp.dma_start(acc_v[q], xin[:, TPC * q:TPC * q + TPC, :]).then_inc(S["acc_put"], 16)

            def store_dd(c):
                for h in range(KC):
                    sp.wait_ge(S["pr_du"], KC * c + h + 1)
                    sp.dma_start(dd_d[D * c + P * h:D * c + P * h + P, :],
                                 prep[c % 2]["dd"][h].rearrange("p k c -> p (k c)")).then_inc(S[f"dd_put{c % 2}{h}"], 16)

            def load_dd(c, g):
                if not (isinstance(c, int) and c == 0 and g < 2):
                    sp.wait_ge(S["exp_done"], unit_index(c, g) - 1)
                    apart(sp)
                    sp.wait_ge(S["dbu_done"], 2 * (unit_index(c, g) - 1))
                apart(sp)
                for q in range(P // DG):
                    sp.dma_start(dd[DG * q:DG * q + DG, g % 2, :, :].rearrange("p k c -> p (k c)"),
                                 dd_d[bass.ds(unit_index(c, g) * DG, DG), :]).then_inc(dd_in[g % 2], 16)

            def load_bc(c, parity, quarters=range(P // DG)):
                for q in quarters:
                    for r in range(2):
                        n = r * NS + NH * q
                        src = bc_d[bass.ds(c, 1), n:n + NH, :].rearrange("o n c -> o (n c)").to_broadcast([DG, NH * CH])
                        sp.dma_start(bc[DG * q:DG * q + DG, parity, r, :, :] if isinstance(parity, int) else
                                     bc[DG * q:DG * q + DG, bass.ds(parity, 1), r, :, :], src).then_inc(S["bc_in"], 16)

            def load_w2():
                for e in range(E):
                    sp.dma_start(w2[:, e * HC * D:(e + 1) * HC * D].rearrange("p (k d) -> p k d", k=HC),
                                 w2_in[e].rearrange("(k p) d -> p k d", p=P)).then_inc(S["w2_in"], 16)

            sp.wait_ge(S["acc_put"], 16 * NCH)
            load_sorted(1)
            xe_v = xe_d.rearrange("(t p) c -> t p c", p=P)

            def load_tile(j, parity, slot):
                v = xe_v[bass.ds(j, 1), :, :].rearrange("o p c -> (o p) c")
                sp.dma_start(xr[:, parity, :], v[:, 0:D]).then_inc(xr_in[parity], 16)
                sp.dma_start(meta[:, slot, :], v[:, D:ROWW]).then_inc(xr_in[parity], 16)

            load_sorted(2)
            for c in range(NCH):
                if c + 3 < NCH:
                    load_sorted(c + 3)
                if c == NCH - 2:
                    sp.wait_ge(S["pr_tr"], NCH - 1)
                    sp.wait_ge(S["pr_ids"], NCH - 1)
                    sp.wait_ge(S["xe_put1"], 16 * NT)
                    sp.wait_ge(S["xe_put2"], 16 * NT)
                    load_tile(0, 0, 0)
                    load_tile(1, 1, 1)
                    load_w2()
                store_dd(c)
                if c == 2:
                    sp.wait_ge(S["bc_put0"], 16)
                    load_bc(0, 0)
                if c == 3:
                    for h in range(KC):
                        sp.wait_ge(S[f"dd_put0{h}"], 16)
                    load_dd(0, 0)
                    load_dd(0, 1)
            for n in range(KC * 2):
                sp.wait_ge(S[f"dd_put{n // 2}{n % 2}"], 16 * NCH // 2)
            for n in range(2):
                sp.wait_ge(S[f"bc_put{n}"], 16 * NCH // 2)

            def turn(c):
                for s in range(SPI):
                    if not (isinstance(c, int) and s < 2):
                        load_dd(c, s)
                    if s == 3:
                        if not isinstance(c, int):
                            sp.wait_ge(S["hc_done"], G * c)
                            apart(sp)
                        sp.wait_ge(S["bc_in"], 128 * (c + 1))
                        if not isinstance(c, int):
                            apart(sp)
                    j = SPI * c + 1 + s
                    sp.wait_ge(S["xtr_done"], j)
                    if not isinstance(c, int):
                        apart(sp)
                    load_tile(j + 1, s % 2, (s + 2) % SPI)
                    if 3 <= s < 3 + P // DG:
                        load_bc((c + 1) % NCH, (c + 1) % 2, [s - 3])

            turn(0)
            with sp.Fori(1, NCH) as c:
                turn(c)
            for j in REST:
                if j + 1 < FT:
                    sp.wait_ge(S["xtr_done"], j)
                    load_tile(j + 1, (j + 1) % 2, (j + 1) % SPI)
            parts = [slice(TPC * D * q, TPC * D * q + TPC * D) for q in range(NCH)]
            sp.wait_ge(S["sum_done"], G * NCH)
            sp.wait_ge(S["yb_put"], 16 * (TPC * NCH + 1))
            for q in range(NCH):
                sp.dma_start(flat[:, parts[q]],
                             acc_d.rearrange("(p r) d -> p (r d)", p=P)[:, parts[q]]).then_inc(S[f"parts_in{q}"], 16)
            sp.wait_ge(S["b_done"], FT)
            sp.wait_ge(S["ye_put"], 16 * (FT + 1))
            for q in range(NCH):
                sp.dma_start(w1[:, parts[q]],
                             y_d[0:TOK, :].rearrange("(p r) d -> p (r d)", p=P)[:, parts[q]]).then_inc(S[f"parts_in{q}"], 16)
            for q in range(NCH):
                sp.wait_ge(S["out_ready"], q + 1)
                sp.dma_start(out.rearrange("b (p r) d -> (b p) (r d)", p=P // BATCH)[:, TPC * D * q:TPC * D * q + TPC * D],
                             w1[:, TPC * D * q:TPC * D * q + TPC * D]).then_inc(S["out_put"], 16)
            sp.wait_ge(S["bc_in"], 128 * (NCH + 1))
            sp.wait_ge(S["out_put"], 16 * NCH)

        @block.gpsimd
        def _(po):
            po.memset(ident[:, :], 0.0).then_inc(S["pool_step"], 1)
            po.memset(fold[:, :], 0.0).then_inc(S["pool_step"], 1)
            po.memset(tri, 1.0).then_inc(S["pool_step"], 1)
            po.wait_ge(S["pool_step"], 3)
            po.affine_select(out=ident[:, :], in_=ident[:, :], compare_op=ALU.not_equal, fill=1.0, base=0,
                             pattern=[[-1, P]], channel_multiplier=1).then_inc(S["pool_const"], 1)
            for q in range(P // DG):
                po.affine_select(out=fold[:, :], in_=fold[:, :], compare_op=ALU.not_equal, fill=1.0, base=-DG * q,
                                 pattern=[[-1, DG]], channel_multiplier=1).then_inc(S["pool_step"], 1)
                po.wait_ge(S["pool_step"], 4 + q)
            po.affine_select(out=tri, in_=tri, compare_op=ALU.is_gt, fill=0.0, base=0,
                             pattern=[[1, P]], channel_multiplier=-1).then_inc(S["pool_const"], 1)
            po.iota(row_u.bitcast(I32)[:, :, D:D + 1], [[P, NT], [0, 1]], base=0, channel_multiplier=1).then_inc(S["pool_const"], 1)
            po.iota(pad.bitcast(I32)[:, D:D + 1], [[0, 1]], base=TOK, channel_multiplier=1).then_inc(S["pad_ready"], 1)
            po.iota(km8, [[1, NB]], base=-NB, channel_multiplier=0, allow_small_or_imprecise_dtypes=True).then_inc(S["pool_const"], 1)
            po.iota(jt, [[1, FTP]], base=0, channel_multiplier=0, allow_small_or_imprecise_dtypes=True).then_inc(S["pool_const"], 1)
            po.iota(c512, [[CH, NCH]], base=0, channel_multiplier=0, allow_small_or_imprecise_dtypes=True).then_inc(S["pool_const"], 1)
            po.iota(iota512[:, :], [[1, CH]], base=0, channel_multiplier=0, allow_small_or_imprecise_dtypes=True).then_inc(S["pool_const"], 1)

            def scatter(dst, index, t, done):
                po.indirect_dma_start(dst[:, :], bass.IndirectOffsetOnAxis(ap=index[:, t:t + 1], axis=0),
                                      row[:, t, 0:dst.shape[1]], None).then_inc(done, 16)

            po.wait_ge(S["pad_ready"], 3)
            for at, name in ((0, "yb_put"), (P // 2, "ye_put")):
                po.dma_start(y_d[TOK + at:TOK + at + P // 2, :], pad[at:at + P // 2, 0:D]).then_inc(S[name], 16)
            po.wait_ge(S["pos_ready"], 1)
            po.wait_ge(S["ln_rows"], NT)
            po.wait_ge(S["pool_const"], 3)
            for t in range(NT):
                scatter(xs_d, pos_a, t, S[f"xs_put{t // (NT // BATCH)}"])
            po.wait_ge(S["ffn_pos_ready"], 1)
            po.wait_ge(S["probs_ready"], 2)
            po.wait_ge(S["pad_put"], 32)
            for t in range(NT):
                scatter(xe_d, pos_1, t, S["xe_put1"])
            po.wait_ge(S["xe_put1"], 16 * NT)
            po.wait_ge(S["xs_put0"], 16 * NT // BATCH)
            po.wait_ge(S["xs_put1"], 16 * NT // BATCH)
            po.tensor_copy(row[:, :, D + 1], prob2[:, :]).then_inc(S["pool_const"], 1)
            po.wait_ge(S["pool_const"], 8)
            for t in range(NT):
                scatter(xe_d, pos_2, t, S["xe_put2"])

            def add_expert(j, slot, parity):
                po.wait_ge(S["ye_done"], j + 2)
                if not isinstance(j, int):
                    apart(po)
                po.wait_ge(S["ye_put"], 16 * (j + 1))
                apart(po)
                po.indirect_dma_start(y_d[:, :], bass.IndirectOffsetOnAxis(ap=meta.bitcast(U32)[:, slot, 0:1], axis=0),
                                      ye[:, parity, :], None, compute_op=ALU.add).then_inc(S["ye_put"], 16)

            def add_scan(c, n):
                po.wait_ge(S["yb_done"], c + 1)
                apart(po)
                po.indirect_dma_start(acc_d[:, :], bass.IndirectOffsetOnAxis(ap=idb[:, n:n + 1], axis=0), yb[:, n, :], None,
                                      compute_op=ALU.add).then_inc(S["yb_put"], 16)

            po.wait_ge(S["acc_put"], 16 * NCH)
            po.wait_ge(S["yb_put"], 16)

            def turn(c):
                for s in range(SPI):
                    po.wait_ge(S["h_ready"], unit_index(c, s) + 1)
                    if isinstance(c, int):
                        c_rows = bc[:, 0, 1, :, :].rearrange("p n c -> p (n c)")
                    else:
                        apart(po)
                        c_rows = bc[:, bass.ds(c % 2, 1), 1, :, :].rearrange("p o n c -> p (o n c)")
                    r = ring[:, s % RING, :, :].rearrange("p n c -> p (n c)")
                    po.tensor_tensor(r, r, c_rows, ALU.mult).then_inc(S["hc_done"], 1)
                    if s in (3, 4, 5, 6) and not isinstance(c, int):
                        add_scan(c - 1, s - 3)
                    add_expert(SPI * c + s, s, s % 2)

            turn(0)
            with po.Fori(1, NCH) as c:
                turn(c)
            for j in REST:
                add_expert(j - 1, (j - 1) % SPI, (j - 1) % 2)
                if j - REST[0] in (2, 3):
                    for n in range(2):
                        add_scan(NCH - 1, 2 * (j - REST[0] - 2) + n)
            add_expert(FT - 1, (FT - 1) % SPI, (FT - 1) % 2)
            po.wait_ge(S["yb_put"], 16 * (TPC * NCH + 1))
            po.wait_ge(S["ye_put"], 16 * (FT + 1))

        @block.scalar
        def _(ac):
            n_const = 0
            for dst, src in ((mnat, means_in), (pnat, prompt_in), (xpnat, xproj_in),
                             (dtnat, dtw_in.rearrange("(k p) r -> p k r", p=P)),
                             *((dtb[:, k:k + 1], dtb_in[P * k:P * k + P].rearrange("(p o) -> p o", o=1)) for k in range(KC)),
                             (wg[:, :, NB:2 * NB], gate_in.rearrange("(k p) e -> p k e", p=P)),
                             (dsb, ds_in.rearrange("(o d) -> o d", o=1).to_broadcast([P, D]))):
                ac.dma_start(dst, src).then_inc(S["const_in"], 16)
                n_const += 16
            for q in range(P // DG):
                ac.dma_start(aneg[DG * q:DG * q + DG, :].rearrange("p (g n) -> p g n", g=G),
                             alog_in.rearrange("(g d) (q n) -> q d g n", d=DG, n=NH)[q]).then_inc(S["const_in"], 16)
                n_const += 16
            assert n_const == 16 * CONST_LOADS
            ac.wait_ge(S["const_in"], n_const)
            ac.wait_ge(S["norm_sq"], 1)
            ac.activation(mrec, msum, ACT.Sqrt).then_inc(S["norm_sqrt"], 1)
            ac.wait_ge(S["small_tr"], 1)
            ac.copy(xprojT[:, :, :].rearrange("p k c -> p (k c)"), pt[:, 0:128]).then_inc(S["small_cp"], 1)
            ac.copy(wg[:, :, 0:NB], pt[:, 128:144].rearrange("p (k r) -> p k r", k=KC)).then_inc(S["small_cp"], 1)
            ac.copy(mT, pt[:, 144:160].rearrange("p (k r) -> p k r", k=KC)).then_inc(S["small_cp"], 1)
            ac.copy(pT, pt[:, 160:192].rearrange("p (k r) -> p k r", k=KC)).then_inc(S["small_cp"], 1)
            ac.copy(dtwT[:, :], pt[0:DTR, 192:448]).then_inc(S["small_cp"], 1)
            ac.wait_ge(S["ln_mm"], 2)
            ac.wait_ge(S["dve_const"], 1)
            ac.copy(cpT[:, DTR + NS:NX], py[0:NB, 0:NS]).then_inc(S["cp_ready"], 1)
            with ac.Fori(0, NCH // 2) as i:
                for h in range(2):
                    q = 2 * i + h
                    ac.wait_ge(S["ln_stats"], q + 1)
                    ac.activation(sd, rt, ACT.Sqrt).then_inc(S["ln_sd"], 1)
                    ac.wait_ge(S["ln_tr"], q + 1)
                    ac.wait_ge(S["ln_mm"], q + 1)
                    for k, src in enumerate((fa[h], fb[h])):
                        ac.copy(xnT[:, h, k, :], src[:, :]).then_inc(S["ln_ev"], 1)
            ac.wait_ge(S["sqrt_v"], 1)
            ac.activation(rn, var, ACT.Sqrt, scale=float(D)).then_inc(S["sqrt_done"], 1)
            ac.wait_ge(S["gap_ready"], 1)
            ac.activation(pr, pr, ACT.Exp).then_inc(S["exp_gap"], 1)
            ac.activation(aneg[:, :], aneg[:, :], ACT.Exp).then_inc(S["aneg_exp"], 1)

            def take_u(c):
                ac.wait_ge(S["pr_tr"], c + 1)
                if c >= 3:
                    ac.wait_ge(S["pr_x"], c - 2)
                    ac.wait_ge(S["pr_du"], KC * (c - 2))
                for k in range(KC):
                    ac.copy(ut[c % 3][:, k, :], rows_ps[c % 2][k]).then_inc(S["pr_ut"], 1)

            def take_x(c):
                xd = prep[c % 2]["xd"]
                ac.wait_ge(S["pr_x"], c + 1)
                if c >= 2:
                    ac.wait_ge(S[f"bc_put{c % 2}"], 16 * (c // 2))
                    ac.wait_ge(S["pr_dp"], KC * (c - 1))
                ac.copy(xd[0:NX, :], x_ps[c % 2][0:NX, :]).then_inc(S["pr_xd"], 1)
                ac.wait_ge(S["pr_xd"], c + 1)
                ac.dma_start(bc_d[c], xd[DTR:NX, :]).then_inc(S[f"bc_put{c % 2}"], 16)

            def softplus_abs(c):
                for h in range(KC):
                    ac.wait_ge(S["pr_dp"], KC * c + h + 1)
                    if c >= 2:
                        ac.wait_ge(S["pr_de"], KC * (c - 2) + h + 1)
                    ac.activation(prep[c % 2]["el"][h], delta_ps[h][:, :], ACT.Abs, bias=dtb[:, h:h + 1]).then_inc(S["pr_ab"], 1)

            def softplus_exp(c):
                for h in range(KC):
                    e = prep[c % 2]["el"][h]
                    ac.wait_ge(S["pr_ab"], KC * c + h + 1)
                    ac.activation(e, e, ACT.Exp, scale=-1.0).then_inc(S["pr_ex"], 1)

            def softplus_ln(c):
                for h in range(KC):
                    e = prep[c % 2]["el"][h]
                    ac.wait_ge(S["pr_ex"], KC * c + h + 1)
                    ac.activation(e, e, ACT.Ln, bias=1.0).then_inc(S["pr_ln"], 1)

            def exps(c, g):
                u = unit_index(c, g)
                ac.wait_ge(dd_in[g % 2], 64 * (c * (G // 2) + g // 2 + 1))
                if isinstance(c, int) and c == 0 and g == 0:
                    for h in range(KC):
                        ac.wait_ge(S[f"dd_put1{h}"], 16 * NCH // 2)
                if not (isinstance(c, int) and c == 0 and g < RING):
                    ac.wait_ge(S["sum_done"], u - RING + 1)
                for n in range(NH):
                    ins = ac.activation(ring[:, g % RING, n, :], dd[:, g % 2, 0, :], ACT.Exp,
                                        scale=aneg[:, NH * g + n:NH * g + n + 1])
                ins.then_inc(S["exp_done"], 1)

            def take_y(c, g, last=False):
                u = unit_index(c, g)
                ac.wait_ge(S["ytr_done"], u + 1)
                if not last:
                    ac.wait_ge(S["sum_done"], u + 2)
                if g == 0 and not (isinstance(c, int) and c == 0):
                    ac.wait_ge(S["yb_done"], c)
                ac.copy(ya[:, :, DG * g:DG * g + DG], pz[:, 384:512].rearrange("p (j d) -> p j d", j=TPC)).then_inc(S["ya_done"], 1)

            def hand_over(c):
                ac.wait_ge(S["ya_done"], G * (c + 1))
                ac.wait_ge(S["yb_put"], 64 * c + 16)
                ac.copy(idb[:, :], ids[:, c * TPC:c * TPC + TPC] if isinstance(c, int) else ids[:, bass.ds(c * TPC, TPC)]).then_inc(S["idb_done"], 1)
                ac.wait_ge(S["idb_done"], c + 1)
                ac.copy(yb[:, :, :].rearrange("p t c -> p (t c)"), ya[:, :, :].rearrange("p t c -> p (t c)")).then_inc(S["yb_done"], 1)

            def take_sum(c, g):
                u = unit_index(c, g)
                ac.wait_ge(S["sum_done"], u + 1)
                if not (isinstance(c, int) and c == 0 and g == 0):
                    ac.wait_ge(S["ytr_done"], u)
                ac.copy(y1[:, :], pz[:, 256:384]).then_inc(S["y1_done"], 1)

            take_u(0)
            take_x(0)
            for c in range(NCH):
                if c + 1 < NCH:
                    take_u(c + 1)
                softplus_abs(c)
                softplus_exp(c)
                if c + 1 < NCH:
                    take_x(c + 1)
                softplus_ln(c)
            ac.wait_ge(S["aneg_exp"], 2)

            def evac_xt(j, parity):
                ac.wait_ge(S["xtr_done"], j + 1)
                ac.copy(xt[:, parity, :], pt[:, 0:D]).then_inc(S["xt_done"], 1)

            def tanh(j, parity):
                ac.wait_ge(S["a_done"], j + 1)
                ac.activation(sg[:, parity, :], fa[parity][:, :], ACT.Tanh, scale=0.5).then_inc(S["tanh_done"], 1)

            def evac_ht(j):
                ac.wait_ge(S["htr_done"], j + 1)
                ac.copy(ht, pt[:, :]).then_inc(S["ht_done"], 1)

            def evac_y(j, parity, slot):
                ac.wait_ge(S["w2_done"], j + 1)
                if not isinstance(j, int) or j >= 2:
                    ac.wait_ge(S["ye_put"], 16 * j)
                ac.activation(ye[:, parity, :], py[:, 0:D], ACT.Copy, scale=meta[:, slot, 1:2]).then_inc(S["ye_done"], 1)

            for n in range(2):
                ac.wait_ge(S[f"bc_put{n}"], 16 * NCH // 2)
            ac.sem_inc(S["ye_done"], 1)
            evac_xt(0, 0)
            tanh(0, 0)
            evac_xt(1, 1)

            def take_units(c, k):
                if k >= 3:
                    take_y(c, k - 3)
                elif not (isinstance(c, int) and c == 0):
                    take_y(c - 1, k + G - 3, last=(isinstance(c, int) and k == 2))
                if k >= 2:
                    if not (isinstance(c, int) and c == NCH):
                        take_sum(c, k - 2)
                elif not (isinstance(c, int) and c == 0):
                    take_sum(c - 1, k + G - 2)

            def turn(c):
                for s in range(SPI):
                    j = SPI * c + 1 + s
                    tanh(j, (s + 1) % 2)
                    evac_ht(j - 1)
                    take_units(c, s)
                    ac.wait_ge(S["b_done"], j)
                    evac_xt(j + 1, s % 2)
                    exps(c, s)
                    if s == 2 and not isinstance(c, int):
                        hand_over(c - 1)
                    evac_y(j - 1, s % 2, s)

            turn(0)
            with ac.Fori(1, NCH) as c:
                turn(c)
            for j in REST:
                tanh(j, j % 2)
                evac_ht(j - 1)
                if j - REST[0] < 3:
                    take_units(NCH, j - REST[0])
                if j + 1 < FT:
                    ac.wait_ge(S["b_done"], j)
                    evac_xt(j + 1, (j + 1) % 2)
                if j - REST[0] == 2:
                    hand_over(NCH - 1)
                evac_y(j - 1, (j - 1) % 2, (j - 1) % SPI)
            evac_ht(FT - 1)
            evac_y(FT - 1, (FT - 1) % 2, (FT - 1) % SPI)

        @block.vector
        def _(ve):
            chained = [0]

            def link(ins, base=0):
                chained[0] += 1
                ins.then_inc(S["chain"], 1)
                ve.wait_ge(S["chain"], base + chained[0])

            ve.memset(pad[:, 0:D], 0.0).then_inc(S["pad_ready"], 1)
            ve.sem_inc(S["acc_ready"], 1)
            ve.memset(pad[:, D + 1:ROWW], 0.0).then_inc(S["pad_ready"], 1)
            ve.memset(ones, 1.0)
            ve.memset(state[:, :], 0.0)
            ve.memset(cpT[:, :], 0.0)
            link(ve.memset(keep[:, :], 1.0))
            ve.memset(keep[:, CPB:CPB + 1], 0.0).then_inc(S["dve_const"], 1)
            ve.wait_ge(S["const_in"], 16 * CONST_LOADS)
            ve.tensor_tensor_reduce(mjunk, mnat, mnat, 1.0, 0.0, ALU.mult, ALU.add, msum).then_inc(S["norm_sq"], 1)
            ve.wait_ge(S["norm_sqrt"], 1)
            link(ve.tensor_scalar(mrec, mrec, EPS_NORM, None, ALU.max))
            link(ve.reciprocal(mrec, mrec))
            ve.tensor_scalar(mnrm, mnat, mrec, None, ALU.mult).then_inc(S["norm_ready"], 1)

            before_ln = chained[0]
            LN_LINKS = 16
            with ve.Fori(0, NCH // 2) as i:
                base = i * LN_LINKS
                for h in range(2):
                    q4 = 8 * i + 4 * h
                    x_t = [xin[:, bass.ds(q4 + t, 1), :].rearrange("p o d -> p (o d)") for t in range(TPC)]
                    ve.wait_ge(x_sem[h], 16 * (i + 1))
                    for t in range(TPC):
                        ins = ve.bn_stats(stats[:, t, :], x_t[t])
                    link(ins, base)
                    apart(ve)
                    for t in range(TPC):
                        ins = ve.bn_aggr(mv[:, t, :], stats[:, t, :])
                    link(ins, base)
                    ve.tensor_copy(var[:, bass.ds(q4, TPC)], mv[:, :, 1])
                    ve.tensor_scalar(rt, mv[:, :, 1], EPS_LN, None, ALU.add).then_inc(S["ln_stats"], 1)
                    ve.wait_ge(S["ln_stats"], 2 * i + h + 1)
                    ve.wait_ge(S["ln_sd"], 2 * i + h + 1)
                    link(ve.reciprocal(rs, sd), base)
                    link(ve.tensor_tensor(sd, rs, rs, ALU.mult), base)
                    link(ve.tensor_tensor(sd, sd, rt, ALU.mult), base)
                    link(ve.tensor_scalar(sd, sd, -0.5, 1.5, ALU.mult, ALU.add), base)
                    link(ve.tensor_tensor(rs, rs, sd, ALU.mult), base)
                    link(ve.tensor_copy(rstd[:, bass.ds(q4, TPC)], rs), base)
                    for t in range(TPC):
                        ve.tensor_scalar(row[:, bass.ds(q4 + t, 1), 0:D].rearrange("p o d -> p (o d)"), x_t[t],
                                         mv[:, t, 0:1], rs[:, t:t + 1], ALU.subtract, ALU.mult).then_inc(S["ln_rows"], 1)
            assert chained[0] - before_ln == LN_LINKS
            chained[0] = before_ln + LN_LINKS * (NCH // 2)
            ve.wait_ge(S["ln_rows"], NT)
            ve.engine_nop().then_inc(S["sqrt_v"], 1)

            def over_k(v):
                return v.rearrange("p (t o) -> p t o", o=1).to_broadcast([P, NT, NB])

            def over_t(v):
                return v.rearrange("p (o k) -> p o k", o=1).to_broadcast([P, NT, NB])

            def first_largest(src, top, onehot):
                link(ve.tensor_reduce(top, src, AX, ALU.max))
                link(ve.tensor_tensor(eq, src, over_k(top), ALU.is_equal))
                link(ve.tensor_tensor(eq, eq, over_t(km8), ALU.mult))
                link(ve.tensor_reduce(mn8, eq, AX, ALU.min))
                link(ve.tensor_tensor(onehot, over_t(km8), over_k(mn8), ALU.is_equal))

            ve.wait_ge(S["ln_mm"], NCH + 2)
            ve.wait_ge(S["pool_const"], 7)
            link(ve.tensor_copy(lg.rearrange("p t c -> p (t c)"), py[:, :]))
            ve.wait_ge(S["sqrt_done"], 1)
            link(ve.tensor_tensor(rn, rn, rstd, ALU.mult))
            link(ve.tensor_scalar(rn, rn, EPS_NORM, None, ALU.max))
            link(ve.reciprocal(rn, rn))
            link(ve.tensor_tensor(sc, lg[:, :, 0:NB], over_k(rn), ALU.mult))
            first_largest(sc, mx, mk[:, 0, :, :])
            ve.engine_nop().then_inc(S["masks_ready"], 1)
            first_largest(lg[:, :, NB:2 * NB], m1, o1)
            link(ve.scalar_tensor_tensor(l2, o1, -BIG, lg[:, :, NB:2 * NB], ALU.mult, ALU.add))

            half = NT * NB
            by_i = dict(b=BATCH, k=NB)

            def tiles_last(v, kind):
                return v[:, 0:half].rearrange("p (b k i) -> p b k i", **by_i) if kind == 0 else \
                    v[:, half:2 * half].rearrange("p (k i) -> p k i", k=NB)

            def running_sum(a):
                link(ve.tensor_tensor_scan(cs[:, a:a + half], ones[:, 0:half], cn[:, a:a + half], 0.0, ALU.mult, ALU.add))
                link(ve.tensor_tensor(ex[:, a:a + half], cs[:, a:a + half], cn[:, a:a + half], ALU.subtract))

            ve.wait_ge(S["ranks_ready"], 1)
            link(ve.tensor_copy(tiles_last(cn, 0), pb[:, half:2 * half].rearrange("p (b i k) -> p b k i", **by_i)))
            running_sum(0)
            link(ve.tensor_tensor(adr[:, 0, :, :].rearrange("p (b i) k -> p b i k", b=BATCH),
                                  pb[:, 0:half].rearrange("p (b i k) -> p b i k", **by_i),
                                  ex[:, 0:half].rearrange("p (b k i) -> p b i k", **by_i), ALU.add))
            link(ve.tensor_tensor(adr[:, 0, :, :], adr[:, 0, :, :], mk[:, 0, :, :], ALU.mult))
            link(ve.tensor_reduce(posf, adr[:, 0, :, :], AX, ALU.add))
            ve.tensor_copy(pos_a[:, :], posf).then_inc(S["pos_ready"], 1)

            first_largest(l2, m2, o2)
            ve.tensor_tensor(pr, m2, m1, ALU.subtract).then_inc(S["gap_ready"], 1)
            link(ve.tensor_tensor(mk[:, 1, :, :], o1, o2, ALU.add))
            ve.engine_nop().then_inc(S["masks_ready"], 1)
            ve.wait_ge(S["exp_gap"], 1)
            link(ve.tensor_scalar(mx, pr, 1.0, None, ALU.add))
            link(ve.reciprocal(mx, mx))
            ve.tensor_copy(row[:, :, D + 1], mx).then_inc(S["probs_ready"], 1)
            ve.tensor_tensor(prob2[:, :], pr, mx, ALU.mult).then_inc(S["probs_ready"], 1)
            ve.wait_ge(S["ranks_ready"], 2)
            link(ve.tensor_copy(tiles_last(cn, 1), pb[:, 3 * half:4 * half].rearrange("p (i k) -> p k i", k=NB)))
            running_sum(half)
            start = tiles_last(ex, 1)[:, :, 0]
            link(ve.tensor_tensor(tl, tiles_last(cs, 1)[:, :, NT - 1], start, ALU.subtract))
            link(ve.tensor_scalar(tli.bitcast(I32), tl, float(P - 1), None, ALU.add))
            link(ve.tensor_scalar(tli.bitcast(I32), tli.bitcast(I32), P.bit_length() - 1, None, ALU.arith_shift_right))
            link(ve.tensor_copy(tl, tli.bitcast(I32)))
            link(ve.tensor_tensor_scan(ct, ones[:, 0:NB], tl, 0.0, ALU.mult, ALU.add))
            link(ve.tensor_tensor(off, ct, tl, ALU.subtract))
            link(ve.scalar_tensor_tensor(off, off, float(P), start, ALU.mult, ALU.subtract))
            link(ve.tensor_tensor(tiles_last(ex, 1), tiles_last(ex, 1),
                                  off.rearrange("p (k o) -> p k o", o=1).to_broadcast([P, NB, NT]), ALU.add))
            link(ve.tensor_tensor(adr[:, 1, :, :], pb[:, 2 * half:3 * half].rearrange("p (i k) -> p i k", k=NB),
                                  ex[:, half:2 * half].rearrange("p (k i) -> p i k", k=NB), ALU.add))
            for onehot, pos in ((o1, pos_1), (o2, pos_2)):
                link(ve.tensor_tensor(eq, adr[:, 1, :, :], onehot, ALU.mult))
                link(ve.tensor_reduce(posf, eq, AX, ALU.add))
                link(ve.tensor_copy(pos[:, :], posf))
            ve.engine_nop().then_inc(S["ffn_pos_ready"], 1)
            last = NB - 1
            link(ve.tensor_tensor(ge[:, :, 0:last], jt.rearrange("p (j o) -> p j o", o=1).to_broadcast([1, FTP, last]),
                                  ct[0:1, 0:last].rearrange("p (o k) -> p o k", o=1).to_broadcast([1, FTP, last]), ALU.is_ge))
            link(ve.tensor_reduce(etf, ge[:, :, 0:last], AX, ALU.add))
            link(ve.tensor_copy(etab[:, :], etf))
            diag = ident[0:NB, 0:NB].rearrange("p (o k) -> p o k", o=1).to_broadcast([NB, BATCH, NB])
            for src, at, one, per_chunk in ((ex, 0, lo1, lo_c), (cs, NT // BATCH - 1, hi1, hi_c)):
                link(ve.tensor_tensor(lo2, src[0:NB, 0:half].rearrange("p (b k i) -> p b k i", **by_i)[:, :, :, at], diag, ALU.mult))
                link(ve.tensor_reduce(one, lo2, AX, ALU.add))
                link(ve.tensor_tensor(per_chunk[:, :].rearrange("p (b c) -> p b c", b=BATCH),
                                      one.rearrange("p (b o) -> p b o", o=1).to_broadcast([NB, BATCH, CPB]),
                                      c512.rearrange("p (b c) -> p b c", b=BATCH), ALU.subtract))

            def cluster_rows(c):
                if c >= 2:
                    ve.wait_ge(S["pr_x"], c - 1)
                if c:
                    ve.wait_ge(S["pr_os"], c)
                osort = prep[c % 2]["osort"]
                link(ve.tensor_scalar(over, iota512[:, :], hi_c[:, c:c + 1], None, ALU.is_ge))
                ve.scalar_tensor_tensor(osort, iota512[:, :], lo_c[:, c:c + 1], over, ALU.is_ge, ALU.subtract).then_inc(S["pr_os"], 1)

            cluster_rows(0)
            cluster_rows(1)
            before_acc = chained[0]
            with ve.Fori(0, NCH) as q:
                x_q = xin[:, bass.ds(TPC * q, TPC), :]
                ve.wait_ge(S["acc_ready"], q + 1)
                link(ve.tensor_tensor(skip, row[:, bass.ds(TPC * q, TPC), 0:D],
                                      dsb.rearrange("p (o d) -> p o d", o=1).to_broadcast([P, TPC, D]), ALU.mult), q)
                ve.tensor_tensor(x_q, x_q, skip, ALU.add).then_inc(S["acc_ready"], 1)
            assert chained[0] - before_acc == 1
            chained[0] = before_acc + NCH
            ve.wait_ge(S["acc_ready"], NCH + 1)
            ve.wait_ge(S["aneg_exp"], 1)
            ve.tensor_scalar(aneg[:, :], aneg[:, :], -1.0, None, ALU.mult).then_inc(S["aneg_exp"], 1)

            def take_ids(c):
                ve.wait_ge(S[f"xs_in{c % 2}"], 16 * (c // 2 + 1))
                ve.tensor_copy(ids[:, TPC * c:TPC * c + TPC], prep[c % 2]["xsr"].bitcast(U32)[:, :, D]).then_inc(S["pr_ids"], 1)

            def prepare(c):
                buf = prep[c % 2]
                if c + 1 < NCH:
                    take_ids(c + 1)
                for h in range(KC):
                    ve.wait_ge(S["pr_ab"], KC * c + h + 1)
                    if c >= 2:
                        ve.wait_ge(S[f"dd_put{c % 2}{h}"], 16 * (c // 2))
                    ve.tensor_scalar(buf["dd"][h][:, 0, :], delta_ps[h][:, :], dtb[:, h:h + 1], 0.0, ALU.add,
                                     ALU.max).then_inc(S["pr_re"], 1)
                if c + 2 < NCH:
                    cluster_rows(c + 2)
                for h in range(KC):
                    n = KC * c + h
                    delta, du = buf["dd"][h][:, 0, :], buf["dd"][h][:, 1, :]
                    ve.wait_ge(S["pr_ln"], n + 1)
                    ve.wait_ge(S["pr_re"], n + 1)
                    ve.tensor_tensor(delta, delta, buf["el"][h], ALU.add).then_inc(S["pr_de"], 1)
                    ve.wait_ge(S["pr_de"], n + 1)
                    ve.wait_ge(S["pr_ut"], KC * (c + 1))
                    ve.tensor_tensor(du, delta, ut[c % 3][:, h, :], ALU.mult).then_inc(S["pr_du"], 1)

            def unit(c, g, parity):
                u = unit_index(c, g)
                ve.wait_ge(dd_in[g % 2], 64 * (c * (G // 2) + g // 2 + 1))
                for half2 in range(2):
                    b_rows = bc[:, parity, 0, 2 * half2:2 * half2 + 2, :] if isinstance(parity, int) else \
                        bc[:, bass.ds(parity, 1), 0, 2 * half2:2 * half2 + 2, :].rearrange("p o n c -> p (o n) c")
                    if not (isinstance(c, int) and c == 0 and g == 0 and half2 == 0):
                        ve.wait_ge(S["scan_done"], 4 * u + 2 * half2)
                    ve.tensor_tensor(pb[:, :].rearrange("p (n c) -> p n c", n=2),
                                     dd[:, g % 2, 1, :].rearrange("p (o c) -> p o c", o=1).to_broadcast([P, 2, CH]),
                                     b_rows, ALU.mult).then_inc(S["dbu_done"], 1)
                    ve.wait_ge(S["dbu_done"], 2 * u + half2 + 1)
                    if half2 == 0:
                        ve.wait_ge(S["exp_done"], u + 1)
                    for m in range(2):
                        n = 2 * half2 + m
                        r = ring[:, g % RING, n, :]
                        ve.tensor_tensor_scan(r, r, pb[:, CH * m:CH * m + CH], state[:, NH * g + n:NH * g + n + 1],
                                              ALU.mult, ALU.add).then_inc(S["scan_done"], 1)
                ve.wait_ge(S["scan_done"], 4 * u + 4)
                ve.tensor_copy(state[:, NH * g:NH * g + NH], ring[:, g % RING, :, CH - 1]).then_inc(S["h_ready"], 1)

            take_ids(0)
            for c in range(NCH):
                prepare(c)

            def silu(j, parity):
                ve.wait_ge(S["tanh_done"], j + 1)
                s = sg[:, parity, :]
                ve.scalar_tensor_tensor(s, s, 1.0, fa[parity][:, :], ALU.add, ALU.mult).then_inc(S["s1_done"], 1)
                ve.wait_ge(S["s1_done"], j + 1)
                ve.wait_ge(S["b_done"], j + 1)
                ve.scalar_tensor_tensor(s, s, 0.5, fb[0][:, :], ALU.mult, ALU.mult).then_inc(S["silu_done"], 1)

            silu(0, 0)

            def turn(c):
                if not isinstance(c, int):
                    ve.wait_ge(S["h_ready"], G * c)
                    ve.tensor_scalar(state[:, :], state[:, :], keep[:, bass.ds(c, 1)], None, ALU.mult).then_inc(S["keep_done"], 1)
                    ve.wait_ge(S["keep_done"], c)
                ve.wait_ge(S["bc_in"], 128 * (c + 1))
                for s in range(SPI):
                    silu(SPI * c + 1 + s, (s + 1) % 2)
                    unit(c, s, c % 2)

            turn(0)
            with ve.Fori(1, NCH) as c:
                turn(c)
            for j in REST:
                silu(j, j % 2)
            for q in range(NCH):
                a, b = [w[:, TPC * D * q:TPC * D * q + TPC * D] for w in (w1, flat)]
                ve.wait_ge(S[f"parts_in{q}"], 32)
                ve.tensor_tensor(a, a, b, ALU.add).then_inc(S["out_ready"], 1)

        @block.tensor
        def _(pe):
            pe.wait_ge(S["const_in"], 16 * CONST_LOADS)
            pe.wait_ge(S["pool_const"], 1)
            pe.wait_ge(S["norm_ready"], 1)
            for k in range(KC):
                cols = slice(P * k, P * k + P)
                pe.transpose(pt[:, NX * k:NX * k + NX], xpnat[:, cols], ident[0:NX, 0:NX])
                pe.transpose(pt[:, 128 + NB * k:136 + NB * k], mnrm[:, cols], ident[0:NB, 0:NB])
                pe.transpose(pt[:, 144 + NB * k:152 + NB * k], mnat[:, cols], ident[0:NB, 0:NB])
                pe.transpose(pt[:, 160 + NS * k:176 + NS * k], pnat[:, cols], ident[0:NS, 0:NS])
                ins = pe.transpose(pt[0:DTR, 192 + P * k:192 + P * k + P], dtnat[:, k, :], ident[:, :])
            ins.then_inc(S["small_tr"], 1)
            pe.wait_ge(S["small_cp"], 5)
            for k in range(KC):
                ins = pe.matmul(py[0:NB, 0:NS], mT[:, k, :], pT[:, k, :], start=(k == 0), stop=(k == KC - 1))
            ins.then_inc(S["ln_mm"], 2)
            pe.wait_ge(S["cp_ready"], 1)
            def turn_tokens(q):
                h = q % 2
                if q > 1:
                    pe.wait_ge(S["ln_ev"], 2 * (q - 1))
                for t in range(TPC):
                    pe.wait_ge(S["ln_rows"], TPC * q + t + 1)
                    for k, dst in enumerate((fa[h], fb[h])):
                        ins = pe.transpose(dst[:, P * t:P * t + P], row[:, TPC * q + t, P * k:P * k + P], ident[:, :])
                ins.then_inc(S["ln_tr"], 1)

            turn_tokens(0)
            for q in range(NCH):
                if q + 1 < NCH:
                    turn_tokens(q + 1)
                pe.wait_ge(S["ln_ev"], 2 * (q + 1))
                for t in range(TPC):
                    col = 16 * (TPC * q + t)
                    for k in range(KC):
                        ins = pe.matmul(py[:, col:col + 16], xnT[:, q % 2, k, P * t:P * t + P], wg[:, k, :],
                                        start=(k == 0), stop=(k == KC - 1))
                ins.then_inc(S["ln_mm"], 1)
            pe.wait_ge(S["pool_const"], 2)
            for kind in range(2):
                pe.wait_ge(S["masks_ready"], kind + 1)
                masks = mk[:, kind, :, :].rearrange("p t k -> p (t k)")
                pe.matmul(pb[:, 512 * kind:512 * kind + 256], tri, masks, start=True, stop=True)
                pe.matmul(pb[:, 512 * kind + 256:512 * kind + 512], ones[:, 0:P], masks, start=True,
                          stop=True).then_inc(S["ranks_ready"], 1)

            def turn_rows(c):
                pe.wait_ge(S[f"xs_in{c % 2}"], 16 * (c // 2 + 1))
                if c == 0:
                    pe.wait_ge(S["ln_ev"], 2 * NCH)
                elif c == 1:
                    pe.wait_ge(S["ffn_pos_ready"], 1)
                else:
                    pe.wait_ge(S["pr_ut"], KC * (c - 1))
                for t in range(TPC):
                    for k in range(KC):
                        ins = pe.transpose(rows_ps[c % 2][k][:, P * t:P * t + P], prep[c % 2]["xsr"][:, t, P * k:P * k + P],
                                           ident[:, :])
                ins.then_inc(S["pr_tr"], 1)

            def project(c):
                buf = prep[c % 2]
                pe.wait_ge(S["pr_ut"], KC * (c + 1))
                pe.wait_ge(S["pr_os"], c + 1)
                if c >= 2:
                    pe.wait_ge(S["pr_xd"], c - 1)
                x_out = x_ps[c % 2][0:NX, :]
                for k in range(KC):
                    pe.matmul(x_out, xprojT[:, k, :], ut[c % 3][:, k, :], start=(k == 0), stop=False)
                pe.matmul(x_out, cpT[:, :], buf["osort"], start=False, stop=True).then_inc(S["pr_x"], 1)

            def project_delta(c):
                pe.wait_ge(S["pr_xd"], c + 1)
                for h in range(KC):
                    if c:
                        pe.wait_ge(S["pr_re"], KC * (c - 1) + h + 1)
                    dst = delta_ps[h]
                    pe.matmul(dst[:, :], dtwT[:, P * h:P * h + P], prep[c % 2]["xd"][0:DTR, :], start=True,
                              stop=True).then_inc(S["pr_dp"], 1)

            def fold_states(c, g):
                u = unit_index(c, g)
                pe.wait_ge(S["hc_done"], u + 1)
                if not (isinstance(c, int) and c == 0 and g == 0):
                    pe.wait_ge(S["y1_done"], u)
                for n in range(NH):
                    for q in range(TPC):
                        ins = pe.matmul(pz[DG * q:DG * q + DG, 256:384], fold[:, :], ring[:, g % RING, n, P * q:P * q + P],
                                        start=(n == 0), stop=(n == NH - 1), tile_position=(0, DG * q))
                ins.then_inc(S["sum_done"], 1)

            def turn_y(c, g):
                u = unit_index(c, g)
                pe.wait_ge(S["y1_done"], u + 1)
                if not (isinstance(c, int) and c == 0 and g == 0):
                    pe.wait_ge(S["ya_done"], u)
                pe.transpose(pz[:, 384:512], y1[:, :], ident[:, :]).then_inc(S["ytr_done"], 1)

            turn_rows(0)
            for c in range(NCH):
                project(c)
                if 0 < c < NCH - 1:
                    turn_rows(c + 1)
                project_delta(c)
                if c == 0:
                    turn_rows(1)

            def turn_x(j, parity, landed):
                pe.wait_ge(xr_in[parity], landed)
                for k in range(KC):
                    ins = pe.transpose(pt[:, P * k:P * k + P], xr[:, parity, P * k:P * k + P], ident[:, :])
                ins.then_inc(S["xtr_done"], 1)

            def expert_of(j):
                apart(pe)
                return pe.value_load(etab[0:1, bass.ds(j, 1)], min_val=0, max_val=E - 1)

            def up(j, parity, e):
                pe.wait_ge(S["xt_done"], j + 1)
                for w, dst, done in ((w1, fa[parity], S["a_done"]), (w3, fb[0], S["b_done"])):
                    if w is w3 and not (isinstance(j, int) and j == 0):
                        pe.wait_ge(S["silu_done"], j)
                    for k in range(KC):
                        ins = pe.matmul(dst[:, :], xt[:, parity, P * k:P * k + P],
                                        w[:, bass.ds(e * (KC * H) + H * k, H)], start=(k == 0), stop=(k == KC - 1))
                    ins.then_inc(done, 1)

            def turn_h(j, parity):
                pe.wait_ge(S["silu_done"], j + 1)
                for k in range(HC):
                    ins = pe.transpose(pt[:, P * k:P * k + P], sg[:, parity, P * k:P * k + P], ident[:, :])
                ins.then_inc(S["htr_done"], 1)

            def down(j, e):
                pe.wait_ge(S["ht_done"], j + 1)
                for k in range(HC):
                    ins = pe.matmul(py[:, 0:D], ht[:, P * k:P * k + P],
                                    w2[:, bass.ds(e * (HC * D) + D * k, D)], start=(k == 0), stop=(k == HC - 1))
                ins.then_inc(S["w2_done"], 1)

            pe.wait_ge(S["pr_de"], KC * NCH)
            pe.wait_ge(S["pr_xd"], NCH)
            pe.wait_ge(S["w13_in"], 16 * 2 * E)
            turn_x(0, 0, 32)
            up(0, 0, expert_of(0))
            turn_x(1, 1, 32)
            pe.wait_ge(S["w2_in"], 16 * E)

            def fold_units(c, k):
                if k >= 3:
                    turn_y(c, k - 3)
                elif not (isinstance(c, int) and c == 0):
                    turn_y(c - 1, k + G - 3)
                if k >= 2:
                    if not (isinstance(c, int) and c == NCH):
                        fold_states(c, k - 2)
                elif not (isinstance(c, int) and c == 0):
                    fold_states(c - 1, k + G - 2)

            def turn(c):
                e_down, e_up = expert_of(SPI * c), expert_of(SPI * c + 1)
                for s in range(SPI):
                    j = SPI * c + 1 + s
                    up(j, (s + 1) % 2, e_up)
                    e_next = expert_of(j + 1) if s + 1 < SPI else None
                    turn_h(j - 1, s % 2)
                    fold_units(c, s)
                    pe.wait_ge(S["ht_done"], j)
                    turn_x(j + 1, s % 2, 32 * (SPI // 2 * c + (s + 2) // 2 + 1))
                    pe.wait_ge(S["ye_done"], j)
                    down(j - 1, e_down)
                    e_down, e_up = e_up, e_next

            turn(0)
            with pe.Fori(1, NCH) as c:
                turn(c)
            e_down, e_up = expert_of(REST[0] - 1), expert_of(REST[0])
            for j in REST:
                up(j, j % 2, e_up)
                e_next = expert_of(j + 1) if j + 1 < FT else None
                turn_h(j - 1, (j - 1) % 2)
                if j - REST[0] < 3:
                    fold_units(NCH, j - REST[0])
                if j + 1 < FT:
                    pe.wait_ge(S["ht_done"], j)
                    turn_x(j + 1, (j + 1) % 2, 32 * ((j + 1) // 2 + 1))
                pe.wait_ge(S["ye_done"], j)
                down(j - 1, e_down)
                e_down, e_up = e_up, e_next
            pe.wait_ge(S["ht_done"], FT - 1)
            turn_h(FT - 1, (FT - 1) % 2)
            pe.wait_ge(S["ye_done"], FT)
            down(FT - 1, e_down)


_INS = ["L0_attn_x", "L0_attn_means", "L0_attn_prompt_weight", "L0_attn_x_proj_weight", "L0_attn_dt_projs_weight",
        "L0_attn_dt_projs_bias", "L0_attn_A_logs", "L0_attn_Ds", "L0_ffn_w_gate", "L0_ffn_w1", "L0_ffn_w3", "L0_ffn_w2"]
_OUTS = [((BATCH, LEN, D), "float32")]


def kernel(**inputs):
    import numpy as _np
    import concourse.bacc as _bacc
    from concourse import mybir as _mybir
    from concourse.bass_utils import run_bass_kernel_spmd as _run

    nc = _bacc.Bacc("TRN2", target_bir_lowering=False, num_devices=1)
    arrays, args = {}, []
    for name in _INS:
        a = _np.ascontiguousarray(inputs[name])
        arrays[f"in_{name}_dram"] = a
        args.append(nc.dram_tensor(f"in_{name}_dram", a.shape, _mybir.dt.from_np(a.dtype), kind="ExternalInput").ap())
    for i, (shape, dtype) in enumerate(_OUTS):
        dt = _mybir.dt.from_np(_np.dtype(dtype))
        args.append(nc.dram_tensor(f"out_{i}_dram", shape, dt, kind="ExternalOutput").ap())
    program(nc, *args)
    r = _run(nc, [arrays], core_ids=[0])
    got = tuple(r.results[0][f"out_{i}_dram"] for i in range(len(_OUTS)))
    return got[0]
```

```python
from contextlib import ExitStack

import concourse.bass as bass
from concourse import mybir

F32 = mybir.dt.float32
U32 = mybir.dt.uint32
I32 = mybir.dt.int32
ALU = mybir.AluOpType
ACT = mybir.ActivationFunctionType
AX = mybir.AxisListType.X

P = 128
BATCH, LEN, D = 2, 2048, 256
TOK = BATCH * LEN
NT = TOK // P
KC = D // P
NB = 8
NS, DTR = 16, 32
NX = DTR + 2 * NS
E, H = 8, 512
HC = H // P
ROWW = D + 2
FT = (2 * TOK) // P + E - 1
FTP = FT + 1
CH = 512
NCH = TOK // CH
CPB = LEN // CH
TPC = CH // P
DG = 32
G = D // DG
NH = 4
RING = 4
SPI = G
SCAN_STEPS = (3, 4, 6, 7)
REST_SCAN_STEPS = (1, 2, 3, 4)
assert len(SCAN_STEPS) == TPC and SCAN_STEPS[-1] == SPI - 1
REST = range(SPI * NCH + 1, FT)
CONST_LOADS, CONST2_LOADS = 5, 7
EPS_LN, EPS_NORM = 1e-5, 1e-12
BIG = 3.0e38


def program(nc, x_in, means_in, prompt_in, xproj_in, dtw_in, dtb_in, alog_in, ds_in, gate_in, w1_in, w3_in, w2_in, out):
    with ExitStack() as ctx:
        def sb(name, shape, dt=F32):
            return ctx.enter_context(nc.sbuf_tensor(name, shape, dt))

        def sem(name):
            return ctx.enter_context(nc.semaphore(name))

        def dram(name, shape):
            return nc.dram_tensor(name, shape, F32, kind="Internal").ap()

        xs_d = dram("xs_d", [TOK, D + 1])
        xe_d = dram("xe_d", [FTP * P, ROWW])
        bc_d = dram("bc_d", [NCH, 2 * NS, CH])
        dd_d = dram("dd_d", [NCH * D, 2 * CH])

        ring = sb("ring", [P, RING, NH, CH])
        bc = sb("bc", [P, 2, 2, NH, CH])
        late = sb("late", [P, 2 * 2 * CH + 2 * TPC * D])
        dd = late[:, 0:2048].rearrange("p (s r c) -> p s r c", s=2, r=2)
        w1 = sb("w1", [P, E * KC * H])
        w3 = sb("w3", [P, E * KC * H])
        w2x = sb("w2x", [P, NT * ROWW])
        w2 = w2x[:, 0:E * HC * D]
        row = w2x[:, :].rearrange("p (t c) -> p t c", c=ROWW)
        row_u = row.bitcast(U32)
        ya = late[:, 2048:3072].rearrange("p (t c) -> p t c", t=TPC)
        yb = late[:, 3072:4096].rearrange("p (t c) -> p t c", t=TPC)
        idb = sb("idb", [P, TPC], U32)
        ids = sb("ids", [P, NT], U32)
        state = sb("state", [P, G * NH])
        keep = sb("keep", [P, NCH])
        aneg = sb("aneg", [P, G * NH])
        ident = sb("ident", [P, P])
        fold = sb("fold", [P, DG])
        y1 = sb("y1", [P, P])
        meta = sb("meta", [P, SPI, 2])
        etab = sb("etab", [1, FTP], I32)

        pool = sb("pool", [P, 5128])
        xr = pool[:, 0:512].rearrange("p (s c) -> p s c", s=2)
        xt = pool[:, 512:1024].rearrange("p (s c) -> p s c", s=2)
        sg = pool[:, 1024:2048].rearrange("p (s c) -> p s c", s=2)
        ht = pool[:, 2048:2560]
        ye = pool[:, 2560:3072].rearrange("p (s c) -> p s c", s=2)
        flat = ring[:, :, :, :].rearrange("p a b c -> p (a b c)")

        def prep_buffers(v, el1, osort):
            return dict(xsr=v[:, 0:TPC * (D + 1)].rearrange("p (t c) -> p t c", c=D + 1),
                        xd=v[:, 2056:2056 + CH // 2], el=[v[:, 2568:3080], el1],
                        dd=[v[:, 3080 + 1024 * h:4104 + 1024 * h].rearrange("p (k c) -> p k c", k=2) for h in range(KC)],
                        osort=osort)

        osort = [sb("osort0", [NB, CH])[:, :], sb("osort1", [NB, CH])[:, :]]
        prep = [prep_buffers(pool, late[:, 3072:3584], osort[0]),
                prep_buffers(flat, flat[:, 5128:5640], osort[1])]
        ut = [v.rearrange("p (k c) -> p k c", k=KC) for v in (pool[:, 1032:2056], flat[:, 1032:2056], flat[:, 6144:7168])]
        over = late[0:NB, 3584:4096]
        iota512 = sb("iota512", [NB, CH])

        xprojT = sb("xprojT", [P, KC, NX])
        dtwT = sb("dtwT", [P, D])
        dtb = sb("dtb", [P, KC])
        cpT = sb("cpT", [NB, NX])
        lo_c = sb("lo_c", [NB, NCH])
        hi_c = sb("hi_c", [NB, NCH])
        prob2 = sb("prob2", [P, NT])
        pos_a = sb("pos_a", [P, NT], U32)
        pos_1 = sb("pos_1", [P, NT], U32)
        pos_2 = sb("pos_2", [P, NT], U32)

        xin = ring[:, :, :, :].rearrange("p a b c -> p (a b c)").rearrange("p (t c) -> p t c", c=D)
        tmp = bc[:, :, :, :, :].rearrange("p a b c d -> p (a b c d)")
        room = [[tmp, 0, 2 * 2 * NH * CH], [late, 0, 4096]]

        def cut(n, parts=P):
            r = room[0] if room[0][1] + n <= room[0][2] else room[1]
            a = r[1]
            r[1] += n
            assert r[1] <= r[2]
            return r[0][0:parts, a:a + n]

        xnT = cut(2 * KC * CH).rearrange("p (s k c) -> p s k c", s=2, k=KC)
        lg = cut(NT * 16).rearrange("p (t c) -> p t c", c=16)
        pad = cut(ROWW)
        dsb = cut(D)
        ones = cut(2 * NB * NT)
        tri = cut(P)
        wg = cut(KC * DG).rearrange("p (k c) -> p k c", k=KC)
        lgT = cut(P)
        nat = cut(D * 3 + 64)
        stats = cut(2 * TPC * 6).rearrange("p (t c) -> p t c", c=6)
        mv = cut(2 * TPC * 2).rearrange("p (t c) -> p t c", c=2)
        sd = cut(2 * TPC)
        rs = cut(2 * TPC)
        rt = cut(2 * TPC)
        mean = cut(NT)
        var = cut(NT)
        rstd = cut(NT)
        rn = cut(NT)
        km8 = cut(NB)
        mk = cut(2 * NT * NB).rearrange("p (a t k) -> p a t k", a=2, k=NB)
        o1 = cut(NT * NB).rearrange("p (t k) -> p t k", k=NB)
        o2 = cut(NT * NB).rearrange("p (t k) -> p t k", k=NB)
        sc = cut(NT * NB).rearrange("p (t k) -> p t k", k=NB)
        l2 = cut(NT * NB).rearrange("p (t k) -> p t k", k=NB)
        eq = cut(NT * NB).rearrange("p (t k) -> p t k", k=NB)
        mx = cut(NT)
        m1 = cut(NT)
        m2 = cut(NT)
        mn8 = cut(NT)
        pr = cut(NT)
        cn = cut(2 * NT * NB)
        cs = cut(2 * NT * NB)
        ex = cut(2 * NT * NB)
        adr = cut(2 * NT * NB).rearrange("p (a t k) -> p a t k", a=2, k=NB)
        tl = cut(NB)
        ct = cut(NB)
        off = cut(NB)
        tli = cut(NB)
        posf = cut(NT)
        jt = cut(FTP, 1)
        ge = cut(FTP * NB, 1).rearrange("p (j k) -> p j k", k=NB)
        etf = cut(FTP, 1)
        lo2 = cut(BATCH * NB, NB).rearrange("p (b k) -> p b k", b=BATCH)
        lo1 = cut(BATCH, NB)
        hi1 = cut(BATCH, NB)
        c512 = cut(NCH, NB)
        mnat = nat[0:NB, 0:D]
        mnrm = nat[0:NB, D:2 * D]
        mjunk = nat[0:NB, 2 * D:3 * D]
        msum = nat[0:NB, 3 * D:3 * D + 1]
        mrec = nat[0:NB, 3 * D + 1:3 * D + 2]
        pnat = cut(D, NS)
        xpnat = cut(D, NX)
        dtnat = cut(KC * DTR).rearrange("p (k r) -> p k r", k=KC)
        mT = cut(KC * NB).rearrange("p (k r) -> p k r", k=KC)
        pT = cut(KC * NS).rearrange("p (k r) -> p k r", k=KC)
        skip = pool[:, 5128 - TPC * D:5128].rearrange("p (t c) -> p t c", c=D)

        def ps(name, cols):
            return ctx.enter_context(nc.psum_tensor(name, [P, cols], F32))

        pb = ps("pb", 1024)
        fa = [ps("fa0", 512), ps("fa1", 512)]
        fb = [ps("fb0", 512), ps("fb1", 512)]
        pz = fb[1]
        pt = ps("pt", 512)
        py = ps("py", 512)
        rows_ps = [(fa[0][:, :], fb[0][:, :]), (pb[:, 0:512], pb[:, 512:1024])]
        x_ps = [fa[1], py]
        delta_ps = [fb[1], pt]

        names = """passed x_in0 x_in1 const_in const2_in pad_ready pad_put w13_in w2_in ln_stats ln_var ln_sd ln_rows0 ln_rows1
        ln_tr ln_ev ln_mm ln_lgt ln_back acc_ready acc_put pool_const dve_const small_tr small_cp cp_ready norm_sq
        norm_sqrt norm_ready sqrt_v sqrt_done chain masks_ready ranks_ready gap_ready exp_gap probs_ready pos_ready
        ffn_pos_ready pool_step xs_put0 xs_put1 xe_put10 xe_put11 xe_put2 aneg_exp xs_in0 xs_in1 pr_tr pr_ut pr_os pr_x
        pr_xd pr_dp0 pr_dp1 pr_dh0 pr_dh1 pr_ab pr_ex pr_ln pr_de pr_du bc_put0 bc_put1 dd_put00 dd_put01 dd_put10
        dd_put11 pr_ids pr_re bc_in dd_in0 dd_in1 exp_done dbu_done scan_done keep_done h_ready hc_done sum_done y1_done
        ytr_done ya_done yb_done idb_done xr_in0 xr_in1 xtr_done xt_done a_done b_done tanh_done s1_done silu_done
        htr_done ht_done w2_done ye_done added""".split()
        S = {n: sem(n) for n in names}
        x_sem = [S["x_in0"], S["x_in1"]]
        dd_in = [S["dd_in0"], S["dd_in1"]]
        xr_in = [S["xr_in0"], S["xr_in1"]]

        block = ctx.enter_context(nc.Block())

        def apart(eng):
            eng.sem_inc(S["passed"], 1)

        def unit_index(chunk, g):
            return chunk * G + g

        def expert_turn(c, s):
            scans = len([m for m in SCAN_STEPS if m <= s])
            if isinstance(c, int) and c == 0:
                return s
            return c * (SPI + TPC) + (s + scans - TPC)

        REST_TURN = SPI * NCH + TPC * (NCH - 1)
        REST_ADDS = []
        for j in range(SPI * NCH, FT):
            REST_ADDS.append(("expert", j))
            REST_ADDS += [("scan", n) for n in range(TPC) if j - SPI * NCH == REST_SCAN_STEPS[n]]

        def landed(turn):
            return (turn + 2) * 16

        @block.sync
        def _(sp):
            x_v = x_in.rearrange("b (q j p) d -> (b q) p j d", p=P, j=TPC)
            for h in range(2):
                sp.dma_start(xin[:, TPC * h:TPC * h + TPC, :], x_v[h]).then_inc(x_sem[h], 16)
            with sp.Fori(1, NCH // 2) as i:
                for h in range(2):
                    sp.wait_ge(x_sem[h], 16 * i)
                    apart(sp)
                    sp.dma_start(xin[:, bass.ds(8 * i + 4 * h, TPC), :],
                                 x_v[bass.ds(2 * i + h, 1), :, :, :].rearrange("o p j d -> (o p) j d")).then_inc(x_sem[h], 16)
            sp.wait_ge(S["pad_ready"], 3)
            sp.dma_start(xe_d.rearrange("(t p) c -> p t c", p=P),
                         pad.rearrange("p (o c) -> p o c", o=1).to_broadcast([P, FTP, ROWW])).then_inc(S["pad_put"], 16)

            def load_w13(e):
                for w, src in ((w1, w1_in), (w3, w3_in)):
                    sp.dma_start(w[:, e * KC * H:(e + 1) * KC * H].rearrange("p (k h) -> p k h", k=KC),
                                 src[e].rearrange("(k p) h -> p k h", p=P)).then_inc(S["w13_in"], 16)

            xs_v = xs_d.rearrange("(q j p) c -> q p j c", p=P, j=TPC)

            def load_sorted(c):
                sp.wait_ge(S[f"xs_put{c // CPB}"], 16 * NT // BATCH)
                if c >= 2:
                    sp.wait_ge(S["pr_tr"], c - 1)
                    sp.wait_ge(S["pr_ids"], c - 1)
                sp.dma_start(prep[c % 2]["xsr"], xs_v[c]).then_inc(S[f"xs_in{c % 2}"], 16)

            acc_v = out[0:TOK, :].rearrange("(q j p) d -> q p j d", p=P, j=TPC)
            for q in range(NCH):
                if q == NCH // 2:
                    for e in range(E):
                        load_w13(e)
                    load_sorted(0)
                sp.wait_ge(S["acc_ready"], q + 2)
                sp.dma_start(acc_v[q], xin[:, TPC * q:TPC * q + TPC, :]).then_inc(S["acc_put"], 16)

            def store_dd(c):
                for h in range(KC):
                    sp.wait_ge(S["pr_du"], KC * c + h + 1)
                    sp.dma_start(dd_d[D * c + P * h:D * c + P * h + P, :],
                                 prep[c % 2]["dd"][h].rearrange("p k c -> p (k c)")).then_inc(S[f"dd_put{c % 2}{h}"], 16)

            def store_bc(c):
                sp.wait_ge(S["pr_xd"], c + 1)
                for n in range(2):
                    sp.dma_start(bc_d[c][:, CH // 2 * n:CH // 2 * n + CH // 2],
                                 prep[c % 2]["xd"][NX * n + DTR:NX * n + NX, :]).then_inc(S[f"bc_put{c % 2}"], 16)

            def load_dd(c, g):
                if not (isinstance(c, int) and c == 0 and g < 2):
                    sp.wait_ge(S["exp_done"], unit_index(c, g) - 1)
                    apart(sp)
                    sp.wait_ge(S["dbu_done"], 2 * (unit_index(c, g) - 1))
                apart(sp)
                for q in range(P // DG):
                    sp.dma_start(dd[DG * q:DG * q + DG, g % 2, :, :].rearrange("p k c -> p (k c)"),
                                 dd_d[bass.ds(unit_index(c, g) * DG, DG), :]).then_inc(dd_in[g % 2], 16)

            def load_bc(c, parity, quarters=range(P // DG)):
                for q in quarters:
                    for r in range(2):
                        n = r * NS + NH * q
                        src = bc_d[bass.ds(c, 1), n:n + NH, :].rearrange("o n c -> o (n c)").to_broadcast([DG, NH * CH])
                        sp.dma_start(bc[DG * q:DG * q + DG, parity, r, :, :] if isinstance(parity, int) else
                                     bc[DG * q:DG * q + DG, bass.ds(parity, 1), r, :, :], src).then_inc(S["bc_in"], 16)

            def load_w2():
                for e in range(E):
                    sp.dma_start(w2[:, e * HC * D:(e + 1) * HC * D].rearrange("p (k d) -> p k d", k=HC),
                                 w2_in[e].rearrange("(k p) d -> p k d", p=P)).then_inc(S["w2_in"], 16)

            sp.wait_ge(S["acc_put"], 16 * NCH)
            load_sorted(1)
            xe_v = xe_d.rearrange("(t p) c -> t p c", p=P)

            def load_tile(j, parity, slot):
                v = xe_v[bass.ds(j, 1), :, :].rearrange("o p c -> (o p) c")
                sp.dma_start(xr[:, parity, :], v[:, 0:D]).then_inc(xr_in[parity], 16)
                sp.dma_start(meta[:, slot, :], v[:, D:ROWW]).then_inc(xr_in[parity], 16)

            load_sorted(2)
            store_bc(0)
            for c in range(NCH):
                if c + 3 < NCH:
                    load_sorted(c + 3)
                if c + 1 < NCH:
                    store_bc(c + 1)
                store_dd(c)
                if c == 2:
                    sp.wait_ge(S["bc_put0"], 32)
                if 2 <= c < 2 + P // DG:
                    load_bc(0, 0, [c - 2])
                if c == 3:
                    for h in range(KC):
                        sp.wait_ge(S[f"dd_put0{h}"], 16)
                    load_dd(0, 0)
                    load_dd(0, 1)
            sp.wait_ge(S["pr_tr"], NCH - 1)
            sp.wait_ge(S["pr_ids"], NCH - 1)
            sp.wait_ge(S["xe_put10"], 16 * NT // 2)
            sp.wait_ge(S["xe_put11"], 16 * NT // 2)
            sp.wait_ge(S["xe_put2"], 16 * NT)
            load_tile(0, 0, 0)
            load_tile(1, 1, 1)
            load_w2()
            for n in range(KC * 2):
                sp.wait_ge(S[f"dd_put{n // 2}{n % 2}"], 16 * NCH // 2)
            for n in range(2):
                sp.wait_ge(S[f"bc_put{n}"], 32 * NCH // 2)

            def turn(c):
                for s in range(SPI):
                    if not (isinstance(c, int) and s < 2):
                        load_dd(c, s)
                    if s == 3:
                        if not isinstance(c, int):
                            sp.wait_ge(S["hc_done"], G * c)
                            apart(sp)
                        sp.wait_ge(S["bc_in"], 128 * (c + 1))
                        if not isinstance(c, int):
                            apart(sp)
                    j = SPI * c + 1 + s
                    sp.wait_ge(S["xtr_done"], j)
                    if not isinstance(c, int):
                        apart(sp)
                    load_tile(j + 1, s % 2, (s + 2) % SPI)
                    if 3 <= s < 3 + P // DG:
                        load_bc((c + 1) % NCH, (c + 1) % 2, [s - 3])

            turn(0)
            with sp.Fori(1, NCH) as c:
                turn(c)
            for j in REST:
                if j + 1 < FT:
                    sp.wait_ge(S["xtr_done"], j)
                    load_tile(j + 1, (j + 1) % 2, (j + 1) % SPI)
            sp.wait_ge(S["bc_in"], 128 * (NCH + 1))

        @block.gpsimd
        def _(po):
            po.memset(ident[:, :], 0.0).then_inc(S["pool_step"], 1)
            po.memset(fold[:, :], 0.0).then_inc(S["pool_step"], 1)
            po.memset(tri, 1.0).then_inc(S["pool_step"], 1)
            po.wait_ge(S["pool_step"], 3)
            po.affine_select(out=ident[:, :], in_=ident[:, :], compare_op=ALU.not_equal, fill=1.0, base=0,
                             pattern=[[-1, P]], channel_multiplier=1).then_inc(S["pool_const"], 1)
            for q in range(P // DG):
                po.affine_select(out=fold[:, :], in_=fold[:, :], compare_op=ALU.not_equal, fill=1.0, base=-DG * q,
                                 pattern=[[-1, DG]], channel_multiplier=1).then_inc(S["pool_step"], 1)
                po.wait_ge(S["pool_step"], 4 + q)
            po.affine_select(out=tri, in_=tri, compare_op=ALU.is_gt, fill=0.0, base=0,
                             pattern=[[1, P]], channel_multiplier=-1).then_inc(S["pool_const"], 1)
            po.iota(row_u.bitcast(I32)[:, :, D:D + 1], [[P, NT], [0, 1]], base=0, channel_multiplier=1).then_inc(S["pool_const"], 1)
            po.iota(pad.bitcast(I32)[:, D:D + 1], [[0, 1]], base=TOK, channel_multiplier=1).then_inc(S["pad_ready"], 1)
            po.iota(km8, [[1, NB]], base=-NB, channel_multiplier=0, allow_small_or_imprecise_dtypes=True).then_inc(S["pool_const"], 1)
            po.iota(jt, [[1, FTP]], base=0, channel_multiplier=0, allow_small_or_imprecise_dtypes=True).then_inc(S["pool_const"], 1)
            po.iota(c512, [[CH, NCH]], base=0, channel_multiplier=0, allow_small_or_imprecise_dtypes=True).then_inc(S["pool_const"], 1)
            po.iota(iota512[:, :], [[1, CH]], base=0, channel_multiplier=0, allow_small_or_imprecise_dtypes=True).then_inc(S["pool_const"], 1)

            def scatter(dst, index, t, done):
                po.indirect_dma_start(dst[:, :], bass.IndirectOffsetOnAxis(ap=index[:, t:t + 1], axis=0),
                                      row[:, t, 0:dst.shape[1]], None).then_inc(done, 16)

            for i in range(NCH // 2):
                po.wait_ge(S["ln_stats"], i + 1)
                for t in range(2 * TPC * i + TPC, 2 * TPC * (i + 1)):
                    po.tensor_scalar(row[:, t, 0:D], xin[:, t, :], mean[:, t:t + 1], rstd[:, t:t + 1], ALU.subtract,
                                     ALU.mult).then_inc(S["ln_rows1"], 1)
            po.wait_ge(S["ln_rows1"], NT // 2)

            po.wait_ge(S["pad_ready"], 3)
            po.dma_start(out[TOK:TOK + P, :], pad[:, 0:D]).then_inc(S["added"], 16)
            po.wait_ge(S["pos_ready"], 1)
            po.wait_ge(S["ln_rows0"], NT // 2)
            po.wait_ge(S["pool_const"], 3)
            for t in range(NT):
                scatter(xs_d, pos_a, t, S[f"xs_put{t // (NT // BATCH)}"])
            po.wait_ge(S["ffn_pos_ready"], 1)
            po.wait_ge(S["probs_ready"], 2)
            po.wait_ge(S["pad_put"], 16)
            for t in range(NT):
                scatter(xe_d, pos_1, t, S[f"xe_put1{t // (NT // 2)}"])
            po.wait_ge(S["xs_put0"], 16 * NT // BATCH)
            po.wait_ge(S["xs_put1"], 16 * NT // BATCH)
            for half in range(2):
                po.wait_ge(S[f"xe_put1{half}"], 16 * NT // 2)
                tiles = range(NT // 2 * half, NT // 2 * (half + 1))
                po.tensor_copy(row[:, tiles.start:tiles.stop, D + 1],
                               prob2[:, tiles.start:tiles.stop]).then_inc(S["pool_const"], 1)
                po.wait_ge(S["pool_const"], 8 + half)
                for t in tiles:
                    scatter(xe_d, pos_2, t, S["xe_put2"])

            def add_expert(turn, j, slot, parity):
                po.wait_ge(S["ye_done"], j + 2)
                if not isinstance(j, int):
                    apart(po)
                po.wait_ge(S["added"], landed(turn - 1))
                apart(po)
                po.indirect_dma_start(out[:, :], bass.IndirectOffsetOnAxis(ap=meta.bitcast(U32)[:, slot, 0:1], axis=0),
                                      ye[:, parity, :], None, compute_op=ALU.add).then_inc(S["added"], 16)

            def add_scan(turn, c, n):
                po.wait_ge(S["yb_done"], c + 1)
                if not isinstance(c, int):
                    apart(po)
                po.wait_ge(S["added"], landed(turn - 1))
                apart(po)
                po.indirect_dma_start(out[:, :], bass.IndirectOffsetOnAxis(ap=idb[:, n:n + 1], axis=0), yb[:, n, :], None,
                                      compute_op=ALU.add).then_inc(S["added"], 16)

            po.wait_ge(S["acc_put"], 16 * NCH)

            def turn(c):
                for s in range(SPI):
                    po.wait_ge(S["h_ready"], unit_index(c, s) + 1)
                    if not isinstance(c, int):
                        apart(po)
                    for half in range(2):
                        states = slice(NH // 2 * half, NH // 2 * (half + 1))
                        c_rows = bc[:, 0, 1, states, :].rearrange("p n c -> p (n c)") if isinstance(c, int) else \
                            bc[:, bass.ds(c % 2, 1), 1, states, :].rearrange("p o n c -> p (o n c)")
                        r = ring[:, s % RING, states, :].rearrange("p n c -> p (n c)")
                        ins = po.tensor_tensor(r, r, c_rows, ALU.mult)
                        if half == 0 and s in SCAN_STEPS and not isinstance(c, int):
                            add_scan(expert_turn(c, s) - 1, c - 1, SCAN_STEPS.index(s))
                    ins.then_inc(S["hc_done"], 1)
                    add_expert(expert_turn(c, s), SPI * c + s, s, s % 2)

            turn(0)
            with po.Fori(1, NCH) as c:
                turn(c)
            for i, (kind, n) in enumerate(REST_ADDS):
                if kind == "expert":
                    add_expert(REST_TURN + i, n, n % SPI, n % 2)
                else:
                    add_scan(REST_TURN + i, NCH - 1, n)
            po.wait_ge(S["added"], landed(REST_TURN + len(REST_ADDS) - 1))

        @block.scalar
        def _(ac):
            for group, name in ((((mnat, means_in), (pnat, prompt_in), (xpnat, xproj_in),
                                  (dtnat, dtw_in.rearrange("(k p) r -> p k r", p=P)),
                                  (wg[:, :, NB:2 * NB], gate_in.rearrange("(k p) e -> p k e", p=P))), "const_in"),
                                ((*((dtb[:, k:k + 1], dtb_in[P * k:P * k + P].rearrange("(p o) -> p o", o=1))
                                    for k in range(KC)),
                                  (dsb, ds_in.rearrange("(o d) -> o d", o=1).to_broadcast([P, D])),
                                  *((aneg[DG * q:DG * q + DG, :].rearrange("p (g n) -> p g n", g=G),
                                     alog_in.rearrange("(g d) (q n) -> q d g n", d=DG, n=NH)[q])
                                    for q in range(P // DG))), "const2_in")):
                for dst, src in group:
                    ac.dma_start(dst, src).then_inc(S[name], 16)
            ac.wait_ge(S["const_in"], 16 * CONST_LOADS)
            ac.wait_ge(S["norm_sq"], 1)
            ac.activation(mrec, msum, ACT.Sqrt).then_inc(S["norm_sqrt"], 1)
            ac.wait_ge(S["small_tr"], 1)
            ac.copy(xprojT[:, :, :].rearrange("p k c -> p (k c)"), pt[:, 0:128]).then_inc(S["small_cp"], 1)
            ac.copy(wg[:, :, 0:NB], pt[:, 128:144].rearrange("p (k r) -> p k r", k=KC)).then_inc(S["small_cp"], 1)
            ac.copy(mT, pt[:, 144:160].rearrange("p (k r) -> p k r", k=KC)).then_inc(S["small_cp"], 1)
            ac.copy(pT, pt[:, 160:192].rearrange("p (k r) -> p k r", k=KC)).then_inc(S["small_cp"], 1)
            for at in (0, NX):
                ac.copy(dtwT[at:at + DTR, :], pt[at:at + DTR, 192:448]).then_inc(S["small_cp"], 1)
            ac.wait_ge(S["ln_mm"], 2)
            ac.wait_ge(S["dve_const"], 1)
            ac.copy(cpT[:, DTR + NS:NX], py[0:NB, 0:NS]).then_inc(S["cp_ready"], 1)
            def deviation(i):
                ac.wait_ge(S["ln_var"], i + 1)
                ac.activation(sd, rt, ACT.Sqrt).then_inc(S["ln_sd"], 1)

            deviation(0)
            for q in range(NCH):
                ac.wait_ge(S["ln_tr"], q + 1)
                if q >= 2:
                    ac.wait_ge(S["ln_mm"], q + 1)
                for k, src in enumerate((fa[q % 2], fb[q % 2])):
                    ac.copy(xnT[:, q % 2, k, :], src[:, :]).then_inc(S["ln_ev"], 1)
                if q % 2 == 0 and q + 2 < NCH:
                    deviation(q // 2 + 1)
                ac.wait_ge(S["ln_mm"], q + 3)
                ac.copy(lgT, pt[:, 0:P]).then_inc(S["ln_lgt"], 1)
            ac.wait_ge(S["sqrt_v"], 1)
            ac.activation(rn, var, ACT.Sqrt, scale=float(D)).then_inc(S["sqrt_done"], 1)
            ac.wait_ge(S["gap_ready"], 1)
            ac.activation(pr, pr, ACT.Exp).then_inc(S["exp_gap"], 1)
            ac.wait_ge(S["const2_in"], 16 * CONST2_LOADS)
            ac.activation(aneg[:, :], aneg[:, :], ACT.Exp).then_inc(S["aneg_exp"], 1)

            def take_u(c):
                ac.wait_ge(S["pr_tr"], c + 1)
                if c >= 3:
                    ac.wait_ge(S["pr_x"], c - 2)
                    ac.wait_ge(S["pr_du"], KC * (c - 2))
                for k in range(KC):
                    ac.copy(ut[c % 3][:, k, :], rows_ps[c % 2][k]).then_inc(S["pr_ut"], 1)

            def take_x(c):
                xd = prep[c % 2]["xd"]
                ac.wait_ge(S["pr_x"], c + 1)
                if c >= 2:
                    ac.wait_ge(S[f"bc_put{c % 2}"], 32 * (c // 2))
                    for h in range(KC):
                        ac.wait_ge(S[f"pr_dp{h}"], c - 1)
                ac.copy(xd, x_ps[c % 2][:, 0:CH // 2]).then_inc(S["pr_xd"], 1)

            def softplus_abs(c):
                for h in range(KC):
                    ac.wait_ge(S[f"pr_dp{h}"], c + 1)
                    if c >= 2:
                        ac.wait_ge(S["pr_de"], KC * (c - 2) + h + 1)
                    ac.activation(prep[c % 2]["el"][h], delta_ps[h][:, :], ACT.Abs, bias=dtb[:, h:h + 1]).then_inc(S["pr_ab"], 1)

            def softplus_exp(c):
                for h in range(KC):
                    e = prep[c % 2]["el"][h]
                    ac.wait_ge(S["pr_ab"], KC * c + h + 1)
                    ac.activation(e, e, ACT.Exp, scale=-1.0).then_inc(S["pr_ex"], 1)

            def softplus_ln(c):
                for h in range(KC):
                    e = prep[c % 2]["el"][h]
                    ac.wait_ge(S["pr_ex"], KC * c + h + 1)
                    ac.activation(e, e, ACT.Ln, bias=1.0).then_inc(S["pr_ln"], 1)

            def exps(c, g):
                u = unit_index(c, g)
                ac.wait_ge(dd_in[g % 2], 64 * (c * (G // 2) + g // 2 + 1))
                if isinstance(c, int) and c == 0 and g == 0:
                    for h in range(KC):
                        ac.wait_ge(S[f"dd_put1{h}"], 16 * NCH // 2)
                if not (isinstance(c, int) and c == 0 and g < RING):
                    ac.wait_ge(S["sum_done"], u - RING + 1)
                for n in range(NH):
                    ins = ac.activation(ring[:, g % RING, n, :], dd[:, g % 2, 0, :], ACT.Exp,
                                        scale=aneg[:, NH * g + n:NH * g + n + 1])
                ins.then_inc(S["exp_done"], 1)

            def take_y(c, g, last=False):
                u = unit_index(c, g)
                ac.wait_ge(S["ytr_done"], u + 1)
                if not last:
                    ac.wait_ge(S["sum_done"], u + 2)
                if g == 0 and not (isinstance(c, int) and c == 0):
                    ac.wait_ge(S["yb_done"], c)
                ac.copy(ya[:, :, DG * g:DG * g + DG], pz[:, 384:512].rearrange("p (j d) -> p j d", j=TPC)).then_inc(S["ya_done"], 1)

            def hand_over(c):
                ac.wait_ge(S["ya_done"], G * (c + 1))
                ac.wait_ge(S["added"], landed(expert_turn(c, SCAN_STEPS[-1]) - 1))
                ac.copy(idb[:, :], ids[:, bass.ds(c * TPC, TPC)]).then_inc(S["idb_done"], 1)
                ac.wait_ge(S["idb_done"], c + 1)
                ac.copy(yb[:, :, :].rearrange("p t c -> p (t c)"), ya[:, :, :].rearrange("p t c -> p (t c)")).then_inc(S["yb_done"], 1)

            def take_sum(c, g):
                u = unit_index(c, g)
                ac.wait_ge(S["sum_done"], u + 1)
                if not (isinstance(c, int) and c == 0 and g == 0):
                    ac.wait_ge(S["ytr_done"], u)
                ac.copy(y1[:, :], pz[:, 256:384]).then_inc(S["y1_done"], 1)

            take_u(0)
            take_x(0)
            for c in range(NCH):
                if c + 1 < NCH:
                    take_u(c + 1)
                softplus_abs(c)
                softplus_exp(c)
                if c + 1 < NCH:
                    take_x(c + 1)
                softplus_ln(c)
            ac.wait_ge(S["aneg_exp"], 2)

            def evac_xt(j, parity, bank=pt):
                ac.wait_ge(S["xtr_done"], j + 1)
                ac.copy(xt[:, parity, :], bank[:, 0:D]).then_inc(S["xt_done"], 1)

            def tanh(j, parity):
                ac.wait_ge(S["a_done"], j + 1)
                ac.activation(sg[:, parity, :], fa[parity][:, :], ACT.Tanh, scale=0.5).then_inc(S["tanh_done"], 1)

            def evac_ht(j):
                ac.wait_ge(S["htr_done"], j + 1)
                ac.copy(ht, pt[:, :]).then_inc(S["ht_done"], 1)

            def evac_y(j, parity, slot, turn):
                ac.wait_ge(S["w2_done"], j + 1)
                if turn is not None:
                    ac.wait_ge(S["added"], landed(turn))
                ac.activation(ye[:, parity, :], py[:, 0:D], ACT.Copy, scale=meta[:, slot, 1:2]).then_inc(S["ye_done"], 1)

            ac.sem_inc(S["ye_done"], 1)
            evac_xt(0, 0)
            tanh(0, 0)
            evac_xt(1, 1)

            def take_units(c, k):
                if k >= 3:
                    take_y(c, k - 3)
                elif not (isinstance(c, int) and c == 0):
                    take_y(c - 1, k + G - 3, last=(isinstance(c, int) and k == 2))
                if k >= 2:
                    if not (isinstance(c, int) and c == NCH):
                        take_sum(c, k - 2)
                elif not (isinstance(c, int) and c == 0):
                    take_sum(c - 1, k + G - 2)

            def turn(c):
                for s in range(SPI):
                    j = SPI * c + 1 + s
                    tanh(j, (s + 1) % 2)
                    evac_ht(j - 1)
                    take_units(c, s)
                    ac.wait_ge(S["b_done"], j)
                    evac_xt(j + 1, s % 2)
                    exps(c, s)
                    if s == 2 and not isinstance(c, int):
                        hand_over(c - 1)
                    evac_y(j - 1, s % 2, s, expert_turn(c, s - 2) if s >= 2 else
                           None if isinstance(c, int) else expert_turn(c - 1, SPI - 1) - (1 - s))

            for n in range(2):
                ac.wait_ge(S[f"bc_put{n}"], 32 * NCH // 2)
            turn(0)
            with ac.Fori(1, NCH) as c:
                turn(c)

            def turn_of(j):
                return REST_TURN + REST_ADDS.index(("expert", j)) if j >= SPI * NCH else expert_turn(NCH - 1, j - SPI * (NCH - 1))

            for j in REST:
                tanh(j, j % 2)
                evac_ht(j - 1)
                if j - REST[0] < 3:
                    take_units(NCH, j - REST[0])
                if j + 1 < FT:
                    ac.wait_ge(S["b_done"], j)
                    evac_xt(j + 1, (j + 1) % 2, pz if j - REST[0] >= 3 else pt)
                if j - REST[0] == 2:
                    hand_over(NCH - 1)
                evac_y(j - 1, (j - 1) % 2, (j - 1) % SPI, turn_of(j - 3))
            evac_ht(FT - 1)
            evac_y(FT - 1, (FT - 1) % 2, (FT - 1) % SPI, turn_of(FT - 3))

        @block.vector
        def _(ve):
            chained = [0]

            def link(ins, base=0):
                chained[0] += 1
                ins.then_inc(S["chain"], 1)
                ve.wait_ge(S["chain"], base + chained[0])

            ve.memset(wg[:, :, 2 * NB:DG], 0.0)
            ve.memset(pad[:, 0:D], 0.0).then_inc(S["pad_ready"], 1)
            ve.sem_inc(S["acc_ready"], 1)
            ve.memset(pad[:, D + 1:ROWW], 0.0).then_inc(S["pad_ready"], 1)
            ve.memset(ones, 1.0)
            ve.memset(state[:, :], 0.0)
            ve.memset(cpT[:, :], 0.0)
            link(ve.memset(keep[:, :], 1.0))
            ve.memset(keep[:, CPB:CPB + 1], 0.0).then_inc(S["dve_const"], 1)
            ve.wait_ge(S["const_in"], 16 * CONST_LOADS)
            ve.tensor_tensor_reduce(mjunk, mnat, mnat, 1.0, 0.0, ALU.mult, ALU.add, msum).then_inc(S["norm_sq"], 1)
            ve.wait_ge(S["norm_sqrt"], 1)
            link(ve.tensor_scalar(mrec, mrec, EPS_NORM, None, ALU.max))
            link(ve.reciprocal(mrec, mrec))
            ve.tensor_scalar(mnrm, mnat, mrec, None, ALU.mult).then_inc(S["norm_ready"], 1)

            before_ln = chained[0]
            LN_LINKS = 7
            with ve.Fori(0, NCH // 2) as i:
                base = i * LN_LINKS
                q8 = 2 * TPC * i
                for h in range(2):
                    ve.wait_ge(x_sem[h], 16 * (i + 1))
                    for t in range(TPC * h, TPC * h + TPC):
                        ins = ve.bn_stats(stats[:, t, :], xin[:, bass.ds(q8 + t, 1), :].rearrange("p o d -> p (o d)"))
                link(ins, base)
                apart(ve)
                for t in range(2 * TPC):
                    ins = ve.bn_aggr(mv[:, t, :], stats[:, t, :])
                link(ins, base)
                ve.tensor_copy(var[:, bass.ds(q8, 2 * TPC)], mv[:, :, 1])
                ve.tensor_copy(mean[:, bass.ds(q8, 2 * TPC)], mv[:, :, 0])
                ve.tensor_scalar(rt, mv[:, :, 1], EPS_LN, None, ALU.add).then_inc(S["ln_var"], 1)
                ve.wait_ge(S["ln_var"], i + 1)
                ve.wait_ge(S["ln_sd"], i + 1)
                link(ve.reciprocal(rs, sd), base)
                link(ve.tensor_tensor(sd, rs, rs, ALU.mult), base)
                link(ve.tensor_tensor(sd, sd, rt, ALU.mult), base)
                link(ve.tensor_scalar(sd, sd, -0.5, 1.5, ALU.mult, ALU.add), base)
                link(ve.tensor_tensor(rs, rs, sd, ALU.mult), base)
                ve.tensor_copy(rstd[:, bass.ds(q8, 2 * TPC)], rs).then_inc(S["ln_stats"], 1)
                for t in range(TPC):
                    ve.tensor_scalar(row[:, bass.ds(q8 + t, 1), 0:D].rearrange("p o d -> p (o d)"),
                                     xin[:, bass.ds(q8 + t, 1), :].rearrange("p o d -> p (o d)"),
                                     mv[:, t, 0:1], rs[:, t:t + 1], ALU.subtract, ALU.mult).then_inc(S["ln_rows0"], 1)
            assert chained[0] - before_ln == LN_LINKS
            chained[0] = before_ln + LN_LINKS * (NCH // 2)
            ve.wait_ge(S["ln_rows0"], NT // 2)
            ve.engine_nop().then_inc(S["sqrt_v"], 1)

            def start_sums(first, end):
                before = chained[0]
                with ve.Fori(first, end) as q:
                    x_q = xin[:, bass.ds(TPC * q, TPC), :]
                    ve.wait_ge(S["acc_ready"], q + 1)
                    link(ve.tensor_tensor(skip, row[:, bass.ds(TPC * q, TPC), 0:D],
                                          dsb.rearrange("p (o d) -> p o d", o=1).to_broadcast([P, TPC, D]), ALU.mult),
                         q - first if first else q)
                    ve.tensor_tensor(x_q, x_q, skip, ALU.add).then_inc(S["acc_ready"], 1)
                chained[0] = before + end - first

            ve.wait_ge(S["const2_in"], 16 * CONST2_LOADS)
            ve.wait_ge(S["ln_rows1"], NT // 4)
            start_sums(0, NCH // 2)
            ve.wait_ge(S["ln_rows1"], NT // 2)

            def over_k(v):
                return v.rearrange("p (t o) -> p t o", o=1).to_broadcast([P, NT, NB])

            def over_t(v):
                return v.rearrange("p (o k) -> p o k", o=1).to_broadcast([P, NT, NB])

            def first_largest(src, top, onehot):
                link(ve.tensor_reduce(top, src, AX, ALU.max))
                link(ve.tensor_tensor(eq, src, over_k(top), ALU.is_equal))
                link(ve.tensor_tensor(eq, eq, over_t(km8), ALU.mult))
                link(ve.tensor_reduce(mn8, eq, AX, ALU.min))
                link(ve.tensor_tensor(onehot, over_t(km8), over_k(mn8), ALU.is_equal))

            ve.wait_ge(S["ln_back"], 1)
            ve.wait_ge(S["pool_const"], 7)
            link(ve.tensor_copy(lg, pb[:, :].rearrange("p (t c) -> p t c", c=DG)[:, :, 0:2 * NB]))
            ve.wait_ge(S["sqrt_done"], 1)
            link(ve.tensor_tensor(rn, rn, rstd, ALU.mult))
            link(ve.tensor_scalar(rn, rn, EPS_NORM, None, ALU.max))
            link(ve.reciprocal(rn, rn))
            link(ve.tensor_tensor(sc, lg[:, :, 0:NB], over_k(rn), ALU.mult))
            first_largest(sc, mx, mk[:, 0, :, :])
            ve.engine_nop().then_inc(S["masks_ready"], 1)
            first_largest(lg[:, :, NB:2 * NB], m1, o1)
            link(ve.scalar_tensor_tensor(l2, o1, -BIG, lg[:, :, NB:2 * NB], ALU.mult, ALU.add))

            half = NT * NB
            by_i = dict(b=BATCH, k=NB)

            def tiles_last(v, kind):
                return v[:, 0:half].rearrange("p (b k i) -> p b k i", **by_i) if kind == 0 else \
                    v[:, half:2 * half].rearrange("p (k i) -> p k i", k=NB)

            def running_sum(a):
                link(ve.tensor_tensor_scan(cs[:, a:a + half], ones[:, 0:half], cn[:, a:a + half], 0.0, ALU.mult, ALU.add))
                link(ve.tensor_tensor(ex[:, a:a + half], cs[:, a:a + half], cn[:, a:a + half], ALU.subtract))

            ve.wait_ge(S["ranks_ready"], 1)
            link(ve.tensor_copy(tiles_last(cn, 0), pb[:, half:2 * half].rearrange("p (b i k) -> p b k i", **by_i)))
            running_sum(0)
            link(ve.tensor_tensor(adr[:, 0, :, :].rearrange("p (b i) k -> p b i k", b=BATCH),
                                  pb[:, 0:half].rearrange("p (b i k) -> p b i k", **by_i),
                                  ex[:, 0:half].rearrange("p (b k i) -> p b i k", **by_i), ALU.add))
            link(ve.tensor_tensor(adr[:, 0, :, :], adr[:, 0, :, :], mk[:, 0, :, :], ALU.mult))
            link(ve.tensor_reduce(posf, adr[:, 0, :, :], AX, ALU.add))
            ve.tensor_copy(pos_a[:, :], posf).then_inc(S["pos_ready"], 1)

            first_largest(l2, m2, o2)
            ve.tensor_tensor(pr, m2, m1, ALU.subtract).then_inc(S["gap_ready"], 1)
            link(ve.tensor_tensor(mk[:, 1, :, :], o1, o2, ALU.add))
            ve.engine_nop().then_inc(S["masks_ready"], 1)
            ve.wait_ge(S["exp_gap"], 1)
            link(ve.tensor_scalar(mx, pr, 1.0, None, ALU.add))
            link(ve.reciprocal(mx, mx))
            ve.tensor_copy(row[:, :, D + 1], mx).then_inc(S["probs_ready"], 1)
            ve.tensor_tensor(prob2[:, :], pr, mx, ALU.mult).then_inc(S["probs_ready"], 1)
            ve.wait_ge(S["ranks_ready"], 2)
            link(ve.tensor_copy(tiles_last(cn, 1), pb[:, 3 * half:4 * half].rearrange("p (i k) -> p k i", k=NB)))
            running_sum(half)
            start = tiles_last(ex, 1)[:, :, 0]
            link(ve.tensor_tensor(tl, tiles_last(cs, 1)[:, :, NT - 1], start, ALU.subtract))
            link(ve.tensor_scalar(tli.bitcast(I32), tl, float(P - 1), None, ALU.add))
            link(ve.tensor_scalar(tli.bitcast(I32), tli.bitcast(I32), P.bit_length() - 1, None, ALU.arith_shift_right))
            link(ve.tensor_copy(tl, tli.bitcast(I32)))
            link(ve.tensor_tensor_scan(ct, ones[:, 0:NB], tl, 0.0, ALU.mult, ALU.add))
            link(ve.tensor_tensor(off, ct, tl, ALU.subtract))
            link(ve.scalar_tensor_tensor(off, off, float(P), start, ALU.mult, ALU.subtract))
            link(ve.tensor_tensor(tiles_last(ex, 1), tiles_last(ex, 1),
                                  off.rearrange("p (k o) -> p k o", o=1).to_broadcast([P, NB, NT]), ALU.add))
            link(ve.tensor_tensor(adr[:, 1, :, :], pb[:, 2 * half:3 * half].rearrange("p (i k) -> p i k", k=NB),
                                  ex[:, half:2 * half].rearrange("p (k i) -> p i k", k=NB), ALU.add))
            for onehot, pos in ((o1, pos_1), (o2, pos_2)):
                link(ve.tensor_tensor(eq, adr[:, 1, :, :], onehot, ALU.mult))
                link(ve.tensor_reduce(posf, eq, AX, ALU.add))
                link(ve.tensor_copy(pos[:, :], posf))
            ve.engine_nop().then_inc(S["ffn_pos_ready"], 1)
            last = NB - 1
            link(ve.tensor_tensor(ge[:, :, 0:last], jt.rearrange("p (j o) -> p j o", o=1).to_broadcast([1, FTP, last]),
                                  ct[0:1, 0:last].rearrange("p (o k) -> p o k", o=1).to_broadcast([1, FTP, last]), ALU.is_ge))
            link(ve.tensor_reduce(etf, ge[:, :, 0:last], AX, ALU.add))
            link(ve.tensor_copy(etab[:, :], etf))
            diag = ident[0:NB, 0:NB].rearrange("p (o k) -> p o k", o=1).to_broadcast([NB, BATCH, NB])
            for src, at, one, per_chunk in ((ex, 0, lo1, lo_c), (cs, NT // BATCH - 1, hi1, hi_c)):
                link(ve.tensor_tensor(lo2, src[0:NB, 0:half].rearrange("p (b k i) -> p b k i", **by_i)[:, :, :, at], diag, ALU.mult))
                link(ve.tensor_reduce(one, lo2, AX, ALU.add))
                link(ve.tensor_tensor(per_chunk[:, :].rearrange("p (b c) -> p b c", b=BATCH),
                                      one.rearrange("p (b o) -> p b o", o=1).to_broadcast([NB, BATCH, CPB]),
                                      c512.rearrange("p (b c) -> p b c", b=BATCH), ALU.subtract))

            def cluster_rows(c):
                if c >= 2:
                    ve.wait_ge(S["pr_x"], c - 1)
                if c:
                    ve.wait_ge(S["pr_os"], c)
                osort = prep[c % 2]["osort"]
                link(ve.tensor_scalar(over, iota512[:, :], hi_c[:, c:c + 1], None, ALU.is_ge))
                ve.scalar_tensor_tensor(osort, iota512[:, :], lo_c[:, c:c + 1], over, ALU.is_ge, ALU.subtract).then_inc(S["pr_os"], 1)

            cluster_rows(0)
            cluster_rows(1)
            start_sums(NCH // 2, NCH)
            ve.wait_ge(S["acc_ready"], NCH + 1)
            ve.wait_ge(S["aneg_exp"], 1)
            ve.tensor_scalar(aneg[:, :], aneg[:, :], -1.0, None, ALU.mult).then_inc(S["aneg_exp"], 1)

            def take_ids(c):
                ve.wait_ge(S[f"xs_in{c % 2}"], 16 * (c // 2 + 1))
                ve.tensor_copy(ids[:, TPC * c:TPC * c + TPC], prep[c % 2]["xsr"].bitcast(U32)[:, :, D]).then_inc(S["pr_ids"], 1)

            def prepare(c):
                buf = prep[c % 2]
                if c + 1 < NCH:
                    take_ids(c + 1)
                for h in range(KC):
                    ve.wait_ge(S["pr_ab"], KC * c + h + 1)
                    if c >= 2:
                        ve.wait_ge(S[f"dd_put{c % 2}{h}"], 16 * (c // 2))
                    ve.tensor_scalar(buf["dd"][h][:, 0, :], delta_ps[h][:, :], dtb[:, h:h + 1], 0.0, ALU.add,
                                     ALU.max).then_inc(S["pr_re"], 1)
                if c + 2 < NCH:
                    cluster_rows(c + 2)
                for h in range(KC):
                    n = KC * c + h
                    delta, du = buf["dd"][h][:, 0, :], buf["dd"][h][:, 1, :]
                    ve.wait_ge(S["pr_ln"], n + 1)
                    ve.wait_ge(S["pr_re"], n + 1)
                    ve.tensor_tensor(delta, delta, buf["el"][h], ALU.add).then_inc(S["pr_de"], 1)
                    ve.wait_ge(S["pr_de"], n + 1)
                    ve.wait_ge(S["pr_ut"], KC * (c + 1))
                    ve.tensor_tensor(du, delta, ut[c % 3][:, h, :], ALU.mult).then_inc(S["pr_du"], 1)

            def unit(c, g, parity):
                u = unit_index(c, g)
                ve.wait_ge(dd_in[g % 2], 64 * (c * (G // 2) + g // 2 + 1))
                for half2 in range(2):
                    b_rows = bc[:, parity, 0, 2 * half2:2 * half2 + 2, :] if isinstance(parity, int) else \
                        bc[:, bass.ds(parity, 1), 0, 2 * half2:2 * half2 + 2, :].rearrange("p o n c -> p (o n) c")
                    if not (isinstance(c, int) and c == 0 and g == 0 and half2 == 0):
                        ve.wait_ge(S["scan_done"], 4 * u + 2 * half2)
                    ve.tensor_tensor(pb[:, :].rearrange("p (n c) -> p n c", n=2),
                                     dd[:, g % 2, 1, :].rearrange("p (o c) -> p o c", o=1).to_broadcast([P, 2, CH]),
                                     b_rows, ALU.mult).then_inc(S["dbu_done"], 1)
                    ve.wait_ge(S["dbu_done"], 2 * u + half2 + 1)
                    if half2 == 0:
                        ve.wait_ge(S["exp_done"], u + 1)
                    for m in range(2):
                        n = 2 * half2 + m
                        r = ring[:, g % RING, n, :]
                        ve.tensor_tensor_scan(r, r, pb[:, CH * m:CH * m + CH], state[:, NH * g + n:NH * g + n + 1],
                                              ALU.mult, ALU.add).then_inc(S["scan_done"], 1)
                ve.wait_ge(S["scan_done"], 4 * u + 4)
                ve.tensor_copy(state[:, NH * g:NH * g + NH], ring[:, g % RING, :, CH - 1]).then_inc(S["h_ready"], 1)

            take_ids(0)
            for c in range(NCH):
                prepare(c)

            def silu(j, parity):
                ve.wait_ge(S["tanh_done"], j + 1)
                s = sg[:, parity, :]
                ve.scalar_tensor_tensor(s, s, 1.0, fa[parity][:, :], ALU.add, ALU.mult).then_inc(S["s1_done"], 1)
                ve.wait_ge(S["s1_done"], j + 1)
                ve.wait_ge(S["b_done"], j + 1)
                ve.scalar_tensor_tensor(s, s, 0.5, fb[0][:, :], ALU.mult, ALU.mult).then_inc(S["silu_done"], 1)

            silu(0, 0)

            def turn(c):
                if not isinstance(c, int):
                    ve.wait_ge(S["h_ready"], G * c)
                    ve.tensor_scalar(state[:, :], state[:, :], keep[:, bass.ds(c, 1)], None, ALU.mult).then_inc(S["keep_done"], 1)
                    ve.wait_ge(S["keep_done"], c)
                ve.wait_ge(S["bc_in"], 128 * (c + 1))
                for s in range(SPI):
                    silu(SPI * c + 1 + s, (s + 1) % 2)
                    unit(c, s, c % 2)

            turn(0)
            with ve.Fori(1, NCH) as c:
                turn(c)
            for j in REST:
                silu(j, j % 2)
        @block.tensor
        def _(pe):
            pe.wait_ge(S["const_in"], 16 * CONST_LOADS)
            pe.wait_ge(S["pool_const"], 1)
            pe.wait_ge(S["norm_ready"], 1)
            for k in range(KC):
                cols = slice(P * k, P * k + P)
                pe.transpose(pt[:, NX * k:NX * k + NX], xpnat[:, cols], ident[0:NX, 0:NX])
                pe.transpose(pt[:, 128 + NB * k:136 + NB * k], mnrm[:, cols], ident[0:NB, 0:NB])
                pe.transpose(pt[:, 144 + NB * k:152 + NB * k], mnat[:, cols], ident[0:NB, 0:NB])
                pe.transpose(pt[:, 160 + NS * k:176 + NS * k], pnat[:, cols], ident[0:NS, 0:NS])
                for at in (0, NX):
                    ins = pe.matmul(pt[at:at + DTR, 192 + P * k:192 + P * k + P], dtnat[:, k, :], ident[:, :], start=True,
                                    stop=True, tile_position=(0, at))
            ins.then_inc(S["small_tr"], 1)
            pe.wait_ge(S["small_cp"], 6)
            for k in range(KC):
                ins = pe.matmul(py[0:NB, 0:NS], mT[:, k, :], pT[:, k, :], start=(k == 0), stop=(k == KC - 1))
            ins.then_inc(S["ln_mm"], 2)
            pe.wait_ge(S["cp_ready"], 1)
            def turn_tokens(q):
                h = q % 2
                if q > 1:
                    pe.wait_ge(S["ln_ev"], 2 * (q - 1))
                for t in range(TPC):
                    pe.wait_ge(S[f"ln_rows{h}"], TPC * (q // 2) + t + 1)
                    for k, dst in enumerate((fa[h], fb[h])):
                        ins = pe.transpose(dst[:, P * t:P * t + P], row[:, TPC * q + t, P * k:P * k + P], ident[:, :])
                ins.then_inc(S["ln_tr"], 1)

            def turn_logits(q):
                pe.wait_ge(S["ln_lgt"], q + 1)
                return pe.transpose(pb[:, P * q:P * q + P], lgT, ident[:, :])

            turn_tokens(0)
            for q in range(NCH):
                if q + 1 < NCH:
                    turn_tokens(q + 1)
                if q:
                    turn_logits(q - 1)
                pe.wait_ge(S["ln_ev"], 2 * (q + 1))
                for k in range(KC):
                    for t in range(TPC):
                        ins = pe.matmul(pt[DG * t:DG * t + DG, 0:P], wg[:, k, :], xnT[:, q % 2, k, P * t:P * t + P],
                                        start=(k == 0), stop=(k == KC - 1), tile_position=(0, DG * t))
                ins.then_inc(S["ln_mm"], 1)
            turn_logits(NCH - 1).then_inc(S["ln_back"], 1)
            pe.wait_ge(S["pool_const"], 2)
            for kind in range(2):
                pe.wait_ge(S["masks_ready"], kind + 1)
                masks = mk[:, kind, :, :].rearrange("p t k -> p (t k)")
                pe.matmul(pb[:, 512 * kind:512 * kind + 256], tri, masks, start=True, stop=True)
                pe.matmul(pb[:, 512 * kind + 256:512 * kind + 512], ones[:, 0:P], masks, start=True,
                          stop=True).then_inc(S["ranks_ready"], 1)

            def turn_rows(c):
                pe.wait_ge(S[f"xs_in{c % 2}"], 16 * (c // 2 + 1))
                if c == 0:
                    pe.wait_ge(S["ln_ev"], 2 * NCH)
                elif c == 1:
                    pe.wait_ge(S["ffn_pos_ready"], 1)
                else:
                    pe.wait_ge(S["pr_ut"], KC * (c - 1))
                for t in range(TPC):
                    for k in range(KC):
                        ins = pe.transpose(rows_ps[c % 2][k][:, P * t:P * t + P], prep[c % 2]["xsr"][:, t, P * k:P * k + P],
                                           ident[:, :])
                ins.then_inc(S["pr_tr"], 1)

            def project(c):
                buf = prep[c % 2]
                pe.wait_ge(S["pr_ut"], KC * (c + 1))
                pe.wait_ge(S["pr_os"], c + 1)
                if c >= 2:
                    pe.wait_ge(S["pr_xd"], c - 1)
                halves = [(slice(NX * n, NX * n + NX), slice(CH // 2 * n, CH // 2 * n + CH // 2)) for n in range(2)]
                for k in range(KC + 1):
                    lhs, rhs = (xprojT[:, k, :], ut[c % 3][:, k, :]) if k < KC else (cpT[:, :], buf["osort"])
                    for to, tokens in halves:
                        ins = pe.matmul(x_ps[c % 2][to, 0:CH // 2], lhs, rhs[:, tokens], start=(k == 0), stop=(k == KC),
                                        tile_position=(0, to.start))
                ins.then_inc(S["pr_x"], 1)

            def project_delta(c):
                pe.wait_ge(S["pr_xd"], c + 1)
                for turn, done in ((0, "pr_dh"), (1, "pr_dp")):
                    for h in range(KC):
                        n = (h + turn) % 2
                        at = NX * n
                        if turn == 0 and c:
                            pe.wait_ge(S["pr_re"], KC * (c - 1) + h + 1)
                        if turn == 1:
                            pe.wait_ge(S[f"pr_dh{h}"], c + 1)
                        pe.matmul(delta_ps[h][:, CH // 2 * n:CH // 2 * n + CH // 2], dtwT[at:at + DTR, P * h:P * h + P],
                                  prep[c % 2]["xd"][at:at + DTR, :], start=True, stop=True,
                                  tile_position=(at, 0)).then_inc(S[f"{done}{h}"], 1)

            def fold_states(c, g):
                u = unit_index(c, g)
                pe.wait_ge(S["hc_done"], u + 1)
                if not (isinstance(c, int) and c == 0 and g == 0):
                    pe.wait_ge(S["y1_done"], u)
                for n in range(NH):
                    for q in range(TPC):
                        ins = pe.matmul(pz[DG * q:DG * q + DG, 256:384], fold[:, :], ring[:, g % RING, n, P * q:P * q + P],
                                        start=(n == 0), stop=(n == NH - 1), tile_position=(0, DG * q))
                ins.then_inc(S["sum_done"], 1)

            def turn_y(c, g):
                u = unit_index(c, g)
                pe.wait_ge(S["y1_done"], u + 1)
                if not (isinstance(c, int) and c == 0 and g == 0):
                    pe.wait_ge(S["ya_done"], u)
                pe.transpose(pz[:, 384:512], y1[:, :], ident[:, :]).then_inc(S["ytr_done"], 1)

            turn_rows(0)
            for c in range(NCH):
                project(c)
                if 0 < c < NCH - 1:
                    turn_rows(c + 1)
                project_delta(c)
                if c == 0:
                    turn_rows(1)

            def turn_x(j, parity, landed, bank=pt):
                pe.wait_ge(xr_in[parity], landed)
                for k in range(KC):
                    ins = pe.transpose(bank[:, P * k:P * k + P], xr[:, parity, P * k:P * k + P], ident[:, :])
                ins.then_inc(S["xtr_done"], 1)

            def expert_of(j):
                apart(pe)
                return pe.value_load(etab[0:1, bass.ds(j, 1)], min_val=0, max_val=E - 1)

            def up(j, parity, e):
                pe.wait_ge(S["xt_done"], j + 1)
                for w, dst, done in ((w1, fa[parity], S["a_done"]), (w3, fb[0], S["b_done"])):
                    if w is w3 and not (isinstance(j, int) and j == 0):
                        pe.wait_ge(S["silu_done"], j)
                    for k in range(KC):
                        ins = pe.matmul(dst[:, :], xt[:, parity, P * k:P * k + P],
                                        w[:, bass.ds(e * (KC * H) + H * k, H)], start=(k == 0), stop=(k == KC - 1))
                    ins.then_inc(done, 1)

            def turn_h(j, parity):
                pe.wait_ge(S["silu_done"], j + 1)
                for k in range(HC):
                    ins = pe.transpose(pt[:, P * k:P * k + P], sg[:, parity, P * k:P * k + P], ident[:, :])
                ins.then_inc(S["htr_done"], 1)

            def down(j, e):
                pe.wait_ge(S["ht_done"], j + 1)
                for k in range(HC):
                    ins = pe.matmul(py[:, 0:D], ht[:, P * k:P * k + P],
                                    w2[:, bass.ds(e * (HC * D) + D * k, D)], start=(k == 0), stop=(k == HC - 1))
                ins.then_inc(S["w2_done"], 1)

            pe.wait_ge(S["pr_de"], KC * NCH)
            pe.wait_ge(S["pr_xd"], NCH)
            pe.wait_ge(S["w13_in"], 16 * 2 * E)
            turn_x(0, 0, 32)
            up(0, 0, expert_of(0))
            turn_x(1, 1, 32)

            def fold_units(c, k):
                if k >= 3:
                    turn_y(c, k - 3)
                elif not (isinstance(c, int) and c == 0):
                    turn_y(c - 1, k + G - 3)
                if k >= 2:
                    if not (isinstance(c, int) and c == NCH):
                        fold_states(c, k - 2)
                elif not (isinstance(c, int) and c == 0):
                    fold_states(c - 1, k + G - 2)

            def turn(c):
                e_down, e_up = expert_of(SPI * c), expert_of(SPI * c + 1)
                for s in range(SPI):
                    j = SPI * c + 1 + s
                    up(j, (s + 1) % 2, e_up)
                    e_next = expert_of(j + 1) if s + 1 < SPI else None
                    turn_h(j - 1, s % 2)
                    fold_units(c, s)
                    pe.wait_ge(S["ht_done"], j)
                    turn_x(j + 1, s % 2, 32 * (SPI // 2 * c + (s + 2) // 2 + 1))
                    pe.wait_ge(S["ye_done"], j)
                    if isinstance(c, int) and s == 0:
                        pe.wait_ge(S["w2_in"], 16 * E)
                    down(j - 1, e_down)
                    e_down, e_up = e_up, e_next

            turn(0)
            with pe.Fori(1, NCH) as c:
                turn(c)
            e_down, e_up = expert_of(REST[0] - 1), expert_of(REST[0])
            for j in REST:
                up(j, j % 2, e_up)
                e_next = expert_of(j + 1) if j + 1 < FT else None
                turn_h(j - 1, (j - 1) % 2)
                if j - REST[0] < 3:
                    fold_units(NCH, j - REST[0])
                if j + 1 < FT:
                    after_scan = j - REST[0] >= 3
                    if after_scan:
                        pe.wait_ge(S["ya_done"], G * NCH)
                    else:
                        pe.wait_ge(S["ht_done"], j)
                    turn_x(j + 1, (j + 1) % 2, 32 * ((j + 1) // 2 + 1), pz if after_scan else pt)
                pe.wait_ge(S["ye_done"], j)
                down(j - 1, e_down)
                e_down, e_up = e_up, e_next
            pe.wait_ge(S["ht_done"], FT - 1)
            turn_h(FT - 1, (FT - 1) % 2)
            pe.wait_ge(S["ye_done"], FT)
            down(FT - 1, e_down)


_INS = ["L0_attn_x", "L0_attn_means", "L0_attn_prompt_weight", "L0_attn_x_proj_weight", "L0_attn_dt_projs_weight",
        "L0_attn_dt_projs_bias", "L0_attn_A_logs", "L0_attn_Ds", "L0_ffn_w_gate", "L0_ffn_w1", "L0_ffn_w3", "L0_ffn_w2"]
_OUTS = [((TOK + P, D), "float32")]


def kernel(**inputs):
    import numpy as _np
    import concourse.bacc as _bacc
    from concourse import mybir as _mybir
    from concourse.bass_utils import run_bass_kernel_spmd as _run

    nc = _bacc.Bacc("TRN2", target_bir_lowering=False, num_devices=1)
    arrays, args = {}, []
    for name in _INS:
        a = _np.ascontiguousarray(inputs[name])
        arrays[f"in_{name}_dram"] = a
        args.append(nc.dram_tensor(f"in_{name}_dram", a.shape, _mybir.dt.from_np(a.dtype), kind="ExternalInput").ap())
    for i, (shape, dtype) in enumerate(_OUTS):
        dt = _mybir.dt.from_np(_np.dtype(dtype))
        args.append(nc.dram_tensor(f"out_{i}_dram", shape, dt, kind="ExternalOutput").ap())
    program(nc, *args)
    r = _run(nc, [arrays], core_ids=[0])
    got = tuple(r.results[0][f"out_{i}_dram"] for i in range(len(_OUTS)))
    return got[0][0:TOK].reshape(BATCH, LEN, D)
```
